# Optimizing a Trainium2 kernel written in Bass

```python
import numpy as np
import jax
import jax.numpy as jnp

def _softmax(x, axis=-1):
    return jax.nn.softmax(x, axis=axis)

def _gelu(x):
    return jax.nn.gelu(x, approximate=True)

def _silu(x):
    return jax.nn.silu(x)

def _sigmoid(x):
    return jax.nn.sigmoid(x)

def _layernorm(x, axis=-1, eps=1e-05):
    m = jnp.mean(x, axis=axis, keepdims=True)
    v = jnp.var(x, axis=axis, keepdims=True)
    return (x - m) / jnp.sqrt(v + eps)

def _scatter_add(tgt, idx, src, axis=0):
    return tgt.at[idx].add(src)

def _segment_sum(src, seg, n):
    return jax.ops.segment_sum(src, seg, n)
kernel_name = 'mk_xattn_ffn_d1_seqx_r8_ba89ab'

def setup_inputs(seed: int=0):
    np.random.seed(seed)
    _w = jnp.asarray

    def _rec_inputs():
        import jax
        import jax.numpy as jnp
        _rk = jax.random.key(seed)
        x = -0.0002928 + 1 * jax.random.normal(jax.random.fold_in(_rk, 1), (8, 128, 256), jnp.float32)
        _lenS = 128 - jax.random.randint(jax.random.fold_in(_rk, 7), (8,), 0, max(1, 128 // 4) + 1, jnp.int32)
        _lenS2 = 128 - jax.random.randint(jax.random.fold_in(_rk, 8), (8,), 0, max(1, 128 // 4) + 1, jnp.int32)
        _ctx_2048P = jax.random.normal(jax.random.fold_in(_rk, 11), (8, 16, 256), jnp.float32)
        _ctx_2048c = jax.random.dirichlet(jax.random.fold_in(_rk, 511), 0.3 * jnp.ones((16,), jnp.float32), (8, 128))
        _ctx_2048t = jnp.einsum('bsk,bkd->bsd', _ctx_2048c, _ctx_2048P)
        _ctx_2048t = _ctx_2048t * jax.lax.rsqrt(jnp.mean(jnp.square(_ctx_2048t)) + 1e-12) * 0.953939
        ctx_2048 = -1.39393e-06 + 0.999914 * (_ctx_2048t + 0.3 * jax.random.normal(jax.random.fold_in(_rk, 611), (8, 128, 256), jnp.float32))
        return (x, ctx_2048)
    x, ctx_2048 = _rec_inputs()

    def _L0_xattn_setup():
        import jax, jax.numpy as jnp
        import numpy as np
        B, S, E, NH = (2, 128, 256, 16)
        DH = E // NH
        EPS = 1e-06

        def _mlstm_forward(q, k, v, Wi, bi, Wf, bf, ln_scale):
            b, s, e = q.shape
            nh = Wi.shape[1]
            dh = e // nh
            x = jnp.concatenate([q, k, v], axis=-1)
            ig = (x @ Wi + bi).transpose(0, 2, 1)[..., None]
            fg = (x @ Wf + bf).transpose(0, 2, 1)[..., None]
            split = lambda t: t.reshape(b, s, nh, dh).transpose(0, 2, 1, 3)
            qh, kh, vh = (split(q), split(k), split(v))
            log_f = jax.nn.log_sigmoid(fg)
            log_f_cum = jnp.concatenate([jnp.zeros((b, nh, 1, 1), q.dtype), jnp.cumsum(log_f, axis=2)], axis=2)
            fg_mat = log_f_cum - jnp.transpose(log_f_cum, (0, 1, 3, 2))
            ltr = jnp.tril(jnp.ones((s, s), dtype=bool))
            log_fg = jnp.where(ltr, fg_mat[:, :, 1:, 1:], -jnp.inf)
            log_D = log_fg + jnp.transpose(ig, (0, 1, 3, 2))
            max_log_D = jnp.max(log_D, axis=-1, keepdims=True)
            D = jnp.exp(log_D - max_log_D)
            qk = jnp.einsum('bhsd,bhtd->bhst', qh, kh) / jnp.sqrt(jnp.asarray(dh, q.dtype))
            C = qk * D
            normalizer = jnp.maximum(jnp.abs(C.sum(-1, keepdims=True)), jnp.exp(-max_log_D))
            Cn = C / (normalizer + EPS)
            h = jnp.einsum('bhst,bhtd->bhsd', Cn, vh)
            mu = h.mean(-1, keepdims=True)
            var = ((h - mu) ** 2).mean(-1, keepdims=True)
            hn = (h - mu) * jax.lax.rsqrt(var + EPS)
            hn = hn * ln_scale.reshape(1, nh, 1, dh)
            return hn.transpose(0, 2, 1, 3).reshape(b, s, e)
        key = jax.random.key(seed)
        ks = jax.random.split(key, 6)
        q = jax.random.normal(ks[0], (B, S, E), dtype=jnp.float32)
        k = jax.random.normal(ks[1], (B, S, E), dtype=jnp.float32)
        v = jax.random.normal(ks[2], (B, S, E), dtype=jnp.float32)
        Wi = jax.random.normal(ks[3], (3 * E, NH), dtype=jnp.float32) * 0.02
        bi = jax.random.normal(ks[4], (NH,), dtype=jnp.float32) * 0.1
        Wf = jax.random.normal(ks[5], (3 * E, NH), dtype=jnp.float32) * 0.02
        bf = jnp.linspace(3.0, 6.0, NH, dtype=jnp.float32)
        ln_scale = jnp.ones((E,), dtype=jnp.float32)
        return {'q': q, 'k': k, 'v': v, 'Wi': Wi, 'bi': bi, 'Wf': Wf, 'bf': bf, 'ln_scale': ln_scale}
    _L0_xattn_all = _L0_xattn_setup()
    _L0_xattn_in = {k: v for k, v in _L0_xattn_all.items() if k in ('Wi', 'bi', 'Wf', 'bf', 'ln_scale')}
    del _L0_xattn_all

    def _L0_ffn_setup():
        import jax, jax.numpy as jnp
        import numpy as np
        B, T, C = (2, 128, 256)
        E, TOPK = (8, 2)
        F_MOE = 176
        F_SHARED = 704
        key = jax.random.key(seed)
        ks = jax.random.split(key, 9)
        s = 0.02
        return {'x': jax.random.normal(ks[0], (B, T, C), dtype=jnp.float32), 'gate_w': jax.random.normal(ks[1], (E, C), dtype=jnp.float32) * s, 'expert_fc1': jax.random.normal(ks[2], (E, F_MOE, C), dtype=jnp.float32) * s, 'expert_fc2': jax.random.normal(ks[3], (E, F_MOE, C), dtype=jnp.float32) * s, 'expert_proj': jax.random.normal(ks[4], (E, C, F_MOE), dtype=jnp.float32) * s, 'shared_fc1': jax.random.normal(ks[5], (F_SHARED, C), dtype=jnp.float32) * s, 'shared_fc2': jax.random.normal(ks[6], (F_SHARED, C), dtype=jnp.float32) * s, 'shared_proj': jax.random.normal(ks[7], (C, F_SHARED), dtype=jnp.float32) * s, 'shared_gate_w': jax.random.normal(ks[8], (1, C), dtype=jnp.float32) * s}
    _L0_ffn_all = _L0_ffn_setup()
    _L0_ffn_in = {k: v for k, v in _L0_ffn_all.items() if k in ('gate_w', 'expert_fc1', 'expert_fc2', 'expert_proj', 'shared_fc1', 'shared_fc2', 'shared_proj', 'shared_gate_w')}
    del _L0_ffn_all
    return {'x': x, 'ctx_2048': ctx_2048, 'L0_xattn_Wi': _L0_xattn_in['Wi'], 'L0_xattn_bi': _L0_xattn_in['bi'], 'L0_xattn_Wf': _L0_xattn_in['Wf'], 'L0_xattn_bf': _L0_xattn_in['bf'], 'L0_xattn_ln_scale': _L0_xattn_in['ln_scale'], 'L0_ffn_gate_w': _L0_ffn_in['gate_w'], 'L0_ffn_expert_fc1': _L0_ffn_in['expert_fc1'], 'L0_ffn_expert_fc2': _L0_ffn_in['expert_fc2'], 'L0_ffn_expert_proj': _L0_ffn_in['expert_proj'], 'L0_ffn_shared_fc1': _L0_ffn_in['shared_fc1'], 'L0_ffn_shared_fc2': _L0_ffn_in['shared_fc2'], 'L0_ffn_shared_proj': _L0_ffn_in['shared_proj'], 'L0_ffn_shared_gate_w': _L0_ffn_in['shared_gate_w']}

def reference(x, ctx_2048, L0_xattn_Wi, L0_xattn_bi, L0_xattn_Wf, L0_xattn_bf, L0_xattn_ln_scale, L0_ffn_gate_w, L0_ffn_expert_fc1, L0_ffn_expert_fc2, L0_ffn_expert_proj, L0_ffn_shared_fc1, L0_ffn_shared_fc2, L0_ffn_shared_proj, L0_ffn_shared_gate_w):
    import jax
    import jax.numpy as jnp

    def _L0_xattn_ref(q, k, v, Wi, bi, Wf, bf, ln_scale):
        import jax, jax.numpy as jnp
        import numpy as np
        B, S, E, NH = (2, 128, 256, 16)
        DH = E // NH
        EPS = 1e-06

        def _mlstm_forward(q, k, v, Wi, bi, Wf, bf, ln_scale):
            b, s, e = q.shape
            nh = Wi.shape[1]
            dh = e // nh
            x = jnp.concatenate([q, k, v], axis=-1)
            ig = (x @ Wi + bi).transpose(0, 2, 1)[..., None]
            fg = (x @ Wf + bf).transpose(0, 2, 1)[..., None]
            split = lambda t: t.reshape(b, s, nh, dh).transpose(0, 2, 1, 3)
            qh, kh, vh = (split(q), split(k), split(v))
            log_f = jax.nn.log_sigmoid(fg)
            log_f_cum = jnp.concatenate([jnp.zeros((b, nh, 1, 1), q.dtype), jnp.cumsum(log_f, axis=2)], axis=2)
            fg_mat = log_f_cum - jnp.transpose(log_f_cum, (0, 1, 3, 2))
            ltr = jnp.tril(jnp.ones((s, s), dtype=bool))
            log_fg = jnp.where(ltr, fg_mat[:, :, 1:, 1:], -jnp.inf)
            log_D = log_fg + jnp.transpose(ig, (0, 1, 3, 2))
            max_log_D = jnp.max(log_D, axis=-1, keepdims=True)
            D = jnp.exp(log_D - max_log_D)
            qk = jnp.einsum('bhsd,bhtd->bhst', qh, kh) / jnp.sqrt(jnp.asarray(dh, q.dtype))
            C = qk * D
            normalizer = jnp.maximum(jnp.abs(C.sum(-1, keepdims=True)), jnp.exp(-max_log_D))
            Cn = C / (normalizer + EPS)
            h = jnp.einsum('bhst,bhtd->bhsd', Cn, vh)
            mu = h.mean(-1, keepdims=True)
            var = ((h - mu) ** 2).mean(-1, keepdims=True)
            hn = (h - mu) * jax.lax.rsqrt(var + EPS)
            hn = hn * ln_scale.reshape(1, nh, 1, dh)
            return hn.transpose(0, 2, 1, 3).reshape(b, s, e)
        return _mlstm_forward(q, k, v, Wi, bi, Wf, bf, ln_scale)

    def _L0_ffn_ref(x, gate_w, expert_fc1, expert_fc2, expert_proj, shared_fc1, shared_fc2, shared_proj, shared_gate_w):
        import jax, jax.numpy as jnp
        import numpy as np
        B, T, C = (2, 128, 256)
        E, TOPK = (8, 2)
        F_MOE = 176
        F_SHARED = 704
        b, t, c = x.shape
        xf = x.reshape(-1, c)
        n = xf.shape[0]
        router = xf @ gate_w.T
        probs = jax.nn.softmax(router.astype(jnp.float32), axis=1).astype(x.dtype)
        top_p, top_i = jax.lax.top_k(probs, TOPK)
        combine = jnp.zeros((n, E), dtype=x.dtype).at[jnp.arange(n)[:, None], top_i].set(top_p)
        h1 = jnp.einsum('nc,efc->enf', xf, expert_fc1)
        h2 = jnp.einsum('nc,efc->enf', xf, expert_fc2)
        h = jax.nn.silu(h1) * h2
        out_e = jnp.einsum('enf,ecf->enc', h, expert_proj)
        y = jnp.einsum('ne,enc->nc', combine, out_e)
        s1 = xf @ shared_fc1.T
        s2 = xf @ shared_fc2.T
        shared = jax.nn.silu(s1) * s2 @ shared_proj.T
        y = y + jax.nn.sigmoid(xf @ shared_gate_w.T) * shared
        return y.reshape(b, t, c)
    x = x + _L0_xattn_ref(_layernorm(x, axis=-1), ctx_2048, ctx_2048, L0_xattn_Wi, L0_xattn_bi, L0_xattn_Wf, L0_xattn_bf, L0_xattn_ln_scale)
    x = x + _L0_ffn_ref(_layernorm(x, axis=-1), L0_ffn_gate_w, L0_ffn_expert_fc1, L0_ffn_expert_fc2, L0_ffn_expert_proj, L0_ffn_shared_fc1, L0_ffn_shared_fc2, L0_ffn_shared_proj, L0_ffn_shared_gate_w)
    return x

_drawn_inputs = setup_inputs


def setup_inputs(seed=0):
    import zlib

    import numpy as np

    out = dict(_drawn_inputs(seed))
    spreads = {'L0_xattn_ln_scale': (1.0, 0.2)}
    factors = {'L0_xattn_bi': 64.0,
     'L0_xattn_Wf': 3.47,
     'L0_ffn_gate_w': 8.0,
     'L0_ffn_expert_fc1': 8.0,
     'L0_ffn_expert_fc2': 8.0,
     'L0_ffn_expert_proj': 8.0,
     'L0_ffn_shared_fc1': 7.201,
     'L0_ffn_shared_fc2': 7.148,
     'L0_ffn_shared_proj': 7.151,
     'L0_ffn_shared_gate_w': 8.0}
    for name, (base, spread) in spreads.items():
        noise = np.random.default_rng([zlib.crc32(name.encode()), seed]).standard_normal(out[name].shape)
        drawn = base * np.exp(spread * noise) if base else spread * noise
        out[name] = jnp.asarray(drawn.astype(out[name].dtype))
    for name, factor in factors.items():
        out[name] = (out[name] * factor).astype(out[name].dtype)
    return out
```

```python
from contextlib import ExitStack

import concourse.bass as bass
from concourse import mybir
import numpy as np

F32, F16, BF16, I32 = mybir.dt.float32, mybir.dt.float16, mybir.dt.bfloat16, mybir.dt.int32
ALU, ACT, AX = mybir.AluOpType, mybir.ActivationFunctionType, mybir.AxisListType

P = 128
B, S, E = 8, 128, 256
NH = 16
DH = E // NH
NEX, FM, FS = 8, 176, 704
GB = 2
NG = B // GB
TOK = GB * S
NPAIR = NH // 2
NC_SH = -(-FS // P)
NC_EX = NEX * FM // P
SLOTS = NC_SH + NC_EX
REST = FS - (NC_SH - 1) * P
UH = 8
UNITS = GB * NH // UH
UW = UH * S
QSCALE = 2.0 ** 11
CSCALE = 2.0 ** -3
OUTSCALE = QSCALE * CSCALE * DH ** 0.5
WSCALE = 2.0 ** 15
LN_EPS, EPS = 1e-5, 1e-6
FAR = 1e30
VW = 52


def rows(c):
    return REST if c == NC_SH - 1 else P


def t_order():
    order = []
    for it in range(NG + 1):
        for k in range(SLOTS):
            if it < NG:
                for b in range(GB):
                    if k == 1 + b:
                        order += [("q", GB * it + b), ("k", GB * it + b)]
                    if k == X2_SLOT[b]:
                        order.append(("x2", GB * it + b))
            if it > 0:
                if k == R_SLOT + 1:
                    order.append(("cT", it - 1))
                if k >= NC_SH and (k - NC_SH) % 2 == 0:
                    order.append(("cw", it - 1, k))
    return {key: n + 1 for n, key in enumerate(order)}


def m_order():
    order = []
    for it in range(NG + 1):
        for k in range(SLOTS):
            if it < NG:
                for b in range(GB):
                    if k == 2 + b:
                        order.append(("gates", GB * it + b))
                if k == 4:
                    order.append(("gT", it))
                if k == 5:
                    order.append(("aT", it))
            if it > 0 and k == 0:
                order += [("logits", GB * (it - 1) + b) for b in range(GB)]
    return {key: n + 1 for n, key in enumerate(order)}


UNIT_SLOT = [6, 8, 10, 12]
N_SLOT = [10, 14]
X2_SLOT = [12, 16]
R_SLOT = 1


def build(nc, x, ctx_in, wg, bias_g, ln_scale, gate_w, up, down, ident, ident16, select, lower, out):
    T_AT, M_AT = t_order(), m_order()
    with ExitStack() as stack:
        def sb(name, shape, dt=F32):
            return stack.enter_context(nc.sbuf_tensor(name, shape, dt))

        def sem(name):
            return stack.enter_context(nc.semaphore(name))

        def bank(name, shape=(P, 512), dt=F32):
            return stack.enter_context(nc.psum_tensor(name, list(shape), dt))

        x_sb = sb("x_sb", [P, B, E])
        ctx_sb = sb("ctx_sb", [P, B, E])
        id32 = sb("id32", [P, P])
        id16 = sb("id16", [P, P], F16)
        sel = sb("sel", [2 * NEX, NC_EX * P], F16)
        low = sb("low", [P, NEX, NEX])
        bias_sb = sb("bias_sb", [P, 2 * NH])
        lnsc = sb("lnsc", [P, E])
        gw = sb("gw", [P, 2, NEX + 1])
        wg_in = sb("wg_in", [P, 3, NPAIR * 2 * NH])
        wg_sb = sb("wg_sb", [P, 2, NPAIR, 3, 2 * NH], BF16)
        wg_r = sb("wg_r", [P, 2, NPAIR, 2 * NH])
        w_up = sb("w_up", [P, SLOTS, 2, 2, P])
        w_dn = sb("w_dn", [P, SLOTS, E])
        half = sb("half", [P, NH])
        ones = sb("ones", [GB * NH, S])

        st6 = sb("st6", [P, 2, 6])
        mv = sb("mv", [P, 2 * B, 2])
        ve = sb("ve", [P, 2 * B, NH])
        rstd = sb("rstd", [P, 2 * B, NH])
        pw = sb("pw", [P, B, 3])
        qs = sb("qs", [P, 2, E])
        q3 = sb("q3", [P, 2, NH, 4, DH], F16)
        k3 = sb("k3", [P, 2, NH, 4, DH], F16)
        v5 = sb("v5", [P, 4, NH, VW], BF16)
        vr = sb("vr", [P, 2, NH, DH])
        qT = sb("qT", [P, 4, NPAIR, S], F16)
        kT = sb("kT", [P, 4, NPAIR, S], F16)
        gred = sb("gred", [P, 2, 2, 2 * NH])
        gt1 = sb("gt1", [P, 2, 2 * NH])
        g_tm = sb("g_tm", [P, 2, 2, GB, NH])
        gT = sb("gT", [GB * NH, 2, S])
        gabs = sb("gabs", [GB * NH, 3, S])
        lf = sb("lf", [GB * NH, 2, S])
        aM = sb("aM", [GB * NH, 2, S])
        Gm = sb("Gm", [GB * NH, 2, S])
        Grow = sb("Grow", [1, GB * NH * S])
        a_tm = sb("a_tm", [P, 2, GB * NH])
        eM = sb("eM", [P, 2, GB * NH])
        Z = sb("Z", [P, 3, UH, S])
        Chi = sb("Chi", [P, 2, UH, S], F16)
        Clo = sb("Clo", [P, 2, UH, S], F16)
        U = sb("U", [P, 2, NH, DH])
        rs = sb("rs", [P, 2, NH])
        nrm = sb("nrm", [P, 2, 4, NH])
        hh = sb("hh", [P, 2, NH, DH])
        hm = sb("hm", [P, 2, NH, DH])
        hsq = sb("hsq", [P, 2, NH, DH])
        hst = sb("hst", [P, 2, 2, NH])
        x1 = sb("x1", [P, B, E])
        x2 = sb("x2", [P, 2, E])
        x2T = sb("x2T", [P, 2, 2, TOK])
        lg = sb("lg", [P, 2, GB, NEX + 1])
        nmx = sb("nmx", [P, 2, GB])
        ex = sb("ex", [P, 2, GB, NEX + 1])
        esum = sb("esum", [P, 2, GB, 2])
        rcp = sb("rcp", [P, 2, GB, 2])
        cmpt = sb("cmpt", [P, 2, 3, GB, NEX * NEX])
        rank = sb("rank", [P, 2, 2, GB, NEX])
        c16 = sb("c16", [P, 2, GB, 2, NEX], F16)
        cT = sb("cT", [2 * NEX, 2, TOK], F16)
        s_ff = sb("s_ff", [P, 2, TOK])
        p_ff = sb("p_ff", [P, 2, TOK])
        h_ff = sb("h_ff", [P, 3, TOK])
        y_sb, o_sb = x_sb, x1

        pT = bank("pT")
        pT16 = pT[:, :].bitcast(F16)
        pM = bank("pM")
        pQK = [bank("pQK0"), bank("pQK1")]
        pPV = bank("pPV")
        pU = [bank("pU0"), bank("pU1")]
        pD = bank("pD")

        in_rows = [sem(f"in_rows{b}") for b in range(B)]
        in_const = sem("in_const")
        in_wg = sem("in_wg")
        in_late = sem("in_late")
        in_up = [sem(f"in_up{c}") for c in range(SLOTS)]
        in_dn = [sem(f"in_dn{c}") for c in range(3)]
        g_row_in = [sem("g_row_in0"), sem("g_row_in1")]
        stored = sem("stored")
        dve_step = sem("dve_step")
        act_step = sem("act_step")
        pool_step = sem("pool_step")
        pool_const = sem("pool_const")
        wg_part = sem("wg_part")
        mean_var = sem("mean_var")
        rstd_ok = sem("rstd_ok")
        q_scaled = sem("q_scaled")
        q_hi = sem("q_hi")
        k_pow = sem("k_pow")
        k_hi = sem("k_hi")
        v_one = sem("v_one")
        v_res = sem("v_res")
        v_two = sem("v_two")
        q_ready = sem("q_ready")
        k_ready = sem("k_ready")
        v_ready = sem("v_ready")
        T_full, T_free = sem("T_full"), sem("T_free")
        M_full, M_free = sem("M_full"), sem("M_free")
        qT_ok, kT_ok = sem("qT_ok"), sem("kT_ok")
        gates_ok = sem("gates_ok")
        gT_ok = sem("gT_ok")
        gln_ok = sem("gln_ok")
        aM_ok = sem("aM_ok")
        a_ok = sem("a_ok")
        z_ok = sem("z_ok")
        D_ok = sem("D_ok")
        qk_ok = sem("qk_ok")
        C_ok = sem("C_ok")
        Chi_ok = sem("Chi_ok")
        Clo_ok = sem("Clo_ok")
        pv_ok = sem("pv_ok")
        pv_used = sem("pv_used")
        x2_ok = sem("x2_ok")
        x2T_ok = sem("x2T_ok")
        lg_ok = sem("lg_ok")
        nmx_ok = sem("nmx_ok")
        ex_ok = sem("ex_ok")
        c16_ok = sem("c16_ok")
        cT_ok = sem("cT_ok")
        up_ok = sem("up_ok")
        s_ok = sem("s_ok")
        h_ok = sem("h_ok")
        dn_used = sem("dn_used")
        y_ok = sem("y_ok")
        o_ok = sem("o_ok")

        block = stack.enter_context(nc.Block())

        def bc(ap, n):
            return ap.unsqueeze(2).to_broadcast([ap.shape[0], ap.shape[1], n])

        def dn_part(c):
            return min(c // 6, 2)

        @block.sync
        def _(sp):
            for b in range(GB):
                sp.dma_start(x_sb[:, b, :], x[b]).then_inc(in_rows[b], 16)
                sp.dma_start(ctx_sb[:, b, :], ctx_in[b]).then_inc(in_rows[b], 16)
            for b in range(GB, B):
                sp.dma_start(x_sb[:, b, :], x[b]).then_inc(in_rows[b], 16)
                sp.dma_start(ctx_sb[:, b, :], ctx_in[b]).then_inc(in_rows[b], 16)
            for c in range(SLOTS):
                sp.dma_start(w_up[:, c], up[c]).then_inc(in_up[c], 16)
                if c in (1, 6, 12):
                    n = (1, 6, 12).index(c)
                    lo, hi = 6 * n, min(6 * n + 6, SLOTS)
                    sp.dma_start(w_dn[:, lo:hi, :], down[:, lo:hi, :]).then_inc(in_dn[n], 16)
            for g in range(NG):
                sp.wait_ge(aM_ok, g + 1)
                if g >= 1:
                    sp.wait_ge(z_ok, UNITS * g)
                sp.dma_start(Grow[0:1, :], Gm[:, g % 2, :]).then_inc(g_row_in[g % 2], 16)
            for b in range(B):
                sp.wait_ge(o_ok, b + 1)
                sp.dma_start(out[b], o_sb[:, b, :]).then_inc(stored, 16)
            sp.wait_ge(stored, 16 * B)

        @block.gpsimd
        def _(pool):
            steps = [0]

            def link(instruction):
                steps[0] += 1
                instruction.then_inc(pool_step, 1)
                pool.wait_ge(pool_step, steps[0])

            pool.memset(half[:, :], -0.5).then_inc(pool_const, 1)
            pool.memset(ones[:, :], 1.0).then_inc(pool_const, 1)
            for p in range(2):
                pool.memset(q3[:, p, :, 3, :], 0.0).then_inc(pool_const, 1)
                pool.memset(k3[:, p, :, 3, :], 0.0).then_inc(pool_const, 1)
            pool.wait_ge(pool_const, 1)

            def norm_rows(n, count, scale):
                pool.wait_ge(mean_var, count)
                link(pool.tensor_scalar(ve[:, n, 0:1], mv[:, n, 1:2], LN_EPS, scale ** -2, ALU.add, ALU.mult))
                pool.tensor_tensor(rstd[:, n, 0:1], ve[:, n, 0:1], half[:, 0:1], ALU.pow).then_inc(rstd_ok, 1)

            def norm_heads(b, count):
                pool.wait_ge(mean_var, count)
                link(pool.tensor_scalar(hst[:, b % 2, 1, :], hst[:, b % 2, 1, :], 1.0 / DH, EPS, ALU.mult, ALU.add))
                pool.tensor_tensor(hst[:, b % 2, 1, :], hst[:, b % 2, 1, :], half[:, :], ALU.pow)\
                    .then_inc(rstd_ok, 1)

            for g in range(NG):
                stats = 6 * g
                for b in range(GB):
                    norm_rows(GB * g + b, stats + b + 1, QSCALE)
                pool.wait_ge(g_row_in[g % 2], 16 * (g // 2 + 1))
                pool.wait_ge(a_ok, g + 1)
                for u in range(UNITS):
                    n = UNITS * g + u
                    z = Z[:, n % 3]
                    if n >= 3:
                        pool.wait_ge(Chi_ok, n - 2)
                        pool.wait_ge(Clo_ok, n - 2)
                    link(pool.partition_broadcast(z.rearrange("p h s -> p (h s)"),
                                                  Grow[0:1, u * UW:(u + 1) * UW], P))
                    link(pool.affine_select(out=z, in_=z, compare_op=ALU.is_ge, fill=FAR, base=0,
                                            pattern=[[0, UH], [1, S]], channel_multiplier=-1))
                    pool.tensor_tensor(z, z, bc(a_tm[:, g % 2, u * UH:(u + 1) * UH], S), ALU.subtract)\
                        .then_inc(z_ok, 1)
                for b in range(GB):
                    norm_heads(GB * g + b, stats + 3 + 2 * b)
                    norm_rows(B + GB * g + b, stats + 4 + 2 * b, 1.0)

        @block.scalar
        def _(act):
            steps = [0]

            def link(instruction):
                steps[0] += 1
                instruction.then_inc(act_step, 1)
                act.wait_ge(act_step, steps[0])

            act.dma_start(id32[:, :], ident).then_inc(in_const, 16)
            act.dma_start(id16[:, :], ident16).then_inc(in_const, 16)
            act.dma_start(wg_in[:, :, :], wg).then_inc(in_wg, 16)
            act.dma_start(bias_sb[:, :], bias_g.partition_broadcast(P)).then_inc(in_wg, 16)
            act.dma_start(lnsc[:, :], ln_scale.partition_broadcast(P)).then_inc(in_late, 16)
            act.dma_start(gw[:, :, :], gate_w).then_inc(in_late, 16)
            act.dma_start(sel[:, :], select).then_inc(in_late, 16)
            act.dma_start(low[:, :, :], lower).then_inc(in_late, 16)

            def operands(b):
                r = b % 2
                act.wait_ge(q_scaled, b + 1)
                if b >= 2:
                    act.wait_ge(T_full, T_AT["k", b - 2])
                q = qs[:, r, :].rearrange("p (h i) -> p h i", i=DH).unsqueeze(2).to_broadcast([P, NH, 2, DH])
                act.activation(q3[:, r, :, 0:2, :], q, ACT.Copy).then_inc(q_hi, 1)
                act.wait_ge(k_pow, b + 1)
                c = ctx_sb[:, b, :].rearrange("p (h i) -> p h i", i=DH)
                act.activation(k3[:, r, :, 0:4:2, :], c.unsqueeze(2).to_broadcast([P, NH, 2, DH]), ACT.Copy,
                               scale=pw[:, b, 2:3]).then_inc(k_hi, 1)
                if b >= 4:
                    act.wait_ge(pv_ok, (b - 3) * 2)
                act.activation(v5[:, b % 4, :, 0:DH], c, ACT.Copy, scale=pw[:, b, 1:2]).then_inc(v_one, 1)
                act.wait_ge(v_res, b + 1)
                act.activation(v5[:, b % 4, :, DH:2 * DH], vr[:, r], ACT.Copy).then_inc(v_two, 1)

            def k_columns(b):
                act.wait_ge(T_full, T_AT["k", b])
                if b >= 4:
                    act.wait_ge(qk_ok, (b - 3) * 4)
                act.activation(kT[:, b % 4].rearrange("p j s -> p (j s)"), pT16, ACT.Copy).then_inc(kT_ok, 1)
                act.wait_ge(kT_ok, b + 1)
                act.sem_inc(T_free, 1)

            def forget_logs(g):
                act.wait_ge(gT_ok, g + 1)
                link(act.activation(gabs[:, 0, :], gT[:, 1, :], ACT.Abs))
                link(act.activation(gabs[:, 1, :], gabs[:, 0, :], ACT.Exp, scale=-1.0))
                act.activation(gabs[:, 2, :], gabs[:, 1, :], ACT.Ln, bias=1.0).then_inc(gln_ok, 1)

            def gate_columns(g):
                act.wait_ge(M_full, M_AT["aT", g])
                if g >= 2:
                    act.wait_ge(z_ok, UNITS * (g - 1))
                act.activation(a_tm[:, g % 2, :], pM[:, 0:GB * NH], ACT.Copy).then_inc(a_ok, 1)
                link(act.activation(eM[:, g % 2, :], pM[:, 64:64 + GB * NH], ACT.Exp, scale=-1.0))
                act.wait_ge(a_ok, g + 1)
                act.sem_inc(M_free, 1)

            def decays(n):
                act.wait_ge(z_ok, n + 1)
                z = Z[:, n % 3].rearrange("p h s -> p (h s)")
                act.activation(z, z, ACT.Exp, scale=-1.0).then_inc(D_ok, 1)

            def high_scores(n):
                act.wait_ge(C_ok, 2 * n + 2)
                if n >= 2:
                    act.wait_ge(pv_ok, n - 1)
                act.activation(Chi[:, n % 2], Z[:, n % 3], ACT.Copy).then_inc(Chi_ok, 1)

            def x2_columns(b):
                act.wait_ge(T_full, T_AT["x2", b])
                g = b // 2
                if g >= 2:
                    act.wait_ge(up_ok, SLOTS * (g - 1))
                o = x2T[:, g % 2, :, (b % 2) * S:(b % 2 + 1) * S]
                act.activation(o, pT[:, 0:2 * S].rearrange("p (k s) -> p k s", k=2), ACT.Copy).then_inc(x2T_ok, 1)
                act.wait_ge(x2T_ok, b + 1)
                act.sem_inc(T_free, 1)

            def route_exps(g):
                act.wait_ge(nmx_ok, g + 1)
                for b in range(GB):
                    act.activation(ex[:, g % 2, b, 0:NEX], lg[:, g % 2, b, 0:NEX], ACT.Exp,
                                   bias=nmx[:, g % 2, b:b + 1], accum_out=esum[:, g % 2, b, 0:1]).then_inc(ex_ok, 1)
                    act.activation(ex[:, g % 2, b, NEX:NEX + 1], lg[:, g % 2, b, NEX:NEX + 1], ACT.Exp,
                                   scale=-1.0).then_inc(ex_ok, 1)

            def silu(g, c):
                n = SLOTS * g + c
                act.wait_ge(up_ok, n + 1)
                if n >= 2:
                    act.wait_ge(h_ok, n - 1)
                m = rows(c)
                act.activation(s_ff[0:m, n % 2, :], pU[n % 2][0:m, 0:TOK], ACT.Silu).then_inc(s_ok, 1)

            for it in range(NG + 1):
                for k in range(SLOTS):
                    if it < NG:
                        if k < GB:
                            operands(GB * it + k)
                        if 1 <= k < 1 + GB:
                            k_columns(GB * it + k - 1)
                        if k == 4:
                            forget_logs(it)
                        if k == 5:
                            gate_columns(it)
                        for u in range(UNITS):
                            if k == UNIT_SLOT[u]:
                                decays(UNITS * it + u)
                            if k == UNIT_SLOT[u] + 1:
                                high_scores(UNITS * it + u)
                        for b in range(GB):
                            if k == X2_SLOT[b]:
                                x2_columns(GB * it + b)
                    if it > 0:
                        if k == R_SLOT:
                            route_exps(it - 1)
                        silu(it - 1, k)

        @block.vector
        def _(dve):
            steps = [0]
            stats = [0]

            def link(instruction):
                steps[0] += 1
                instruction.then_inc(dve_step, 1)
                dve.wait_ge(dve_step, steps[0])

            def gate_weights():
                dve.wait_ge(in_wg, 32)
                wi = wg_in[:, :, :].rearrange("p w (j n) -> p w j n", j=NPAIR)
                link(dve.tensor_tensor(wi[:, 1], wi[:, 1], wi[:, 2], ALU.add))
                link(dve.tensor_copy(wg_sb[:, :, :, 0, :], wi[:, 0:2]))
                link(dve.tensor_tensor(wg_r[:, :, :, :], wi[:, 0:2], wg_sb[:, :, :, 0, :], ALU.subtract))
                link(dve.tensor_copy(wg_sb[:, :, :, 1, :], wg_r[:, :, :, :]))
                dve.tensor_tensor(wg_sb[:, :, :, 2, :], wg_r[:, :, :, :], wg_sb[:, :, :, 1, :], ALU.subtract)\
                    .then_inc(wg_part, 1)

            def row_stats(n, source):
                link(dve.bn_stats(st6[:, 0, :], source))
                dve.bn_aggr(mv[:, n, :], st6[:, 0, :]).then_inc(mean_var, 1)
                stats[0] += 1
                dve.wait_ge(mean_var, stats[0])
                dve.wait_ge(rstd_ok, stats[0])

            def operands(b):
                r = b % 2
                dve.wait_ge(in_rows[b], 32)
                link(dve.tensor_reduce(pw[:, b, 0:1], ctx_sb[:, b, :], AX.X, ALU.max, apply_absolute_value=True))
                link(dve.tensor_scalar(pw[:, b, 0:1], pw[:, b, 0:1], 1e-30, None, ALU.max))
                link(dve.tensor_scalar(pw[:, b, 1:2].bitcast(I32), pw[:, b, 0:1].bitcast(I32), 0x7F800000, None,
                                       ALU.bitwise_and))
                dve.reciprocal(pw[:, b, 2:3], pw[:, b, 1:2]).then_inc(k_pow, 1)
                dve.wait_ge(k_pow, b + 1)
                row_stats(b, x_sb[:, b, :])
                if b >= 2:
                    dve.wait_ge(q_hi, b - 1)
                dve.tensor_scalar(qs[:, r, :], x_sb[:, b, :], mv[:, b, 0:1], rstd[:, b, 0:1],
                                  ALU.subtract, ALU.mult).then_inc(q_scaled, 1)
                c = ctx_sb[:, b, :].rearrange("p (h i) -> p h i", i=DH)
                dve.wait_ge(k_hi, b + 1)
                dve.scalar_tensor_tensor(out=k3[:, r, :, 1, :], in0=c, scalar=pw[:, b, 2:3], in1=k3[:, r, :, 0, :],
                                         op0=ALU.mult, op1=ALU.subtract).then_inc(k_ready, 1)
                dve.wait_ge(v_one, b + 1)
                if b >= 2:
                    dve.wait_ge(v_ready, b - 1)
                dve.scalar_tensor_tensor(out=vr[:, r], in0=c, scalar=pw[:, b, 1:2], in1=v5[:, b % 4, :, 0:DH],
                                         op0=ALU.mult, op1=ALU.subtract).then_inc(v_res, 1)
                q = qs[:, r, :].rearrange("p (h i) -> p h i", i=DH)
                dve.wait_ge(q_hi, b + 1)
                dve.wait_ge(q_scaled, b + 1)
                dve.tensor_tensor(q3[:, r, :, 2, :], q, q3[:, r, :, 0, :], ALU.subtract).then_inc(q_ready, 1)
                dve.tensor_copy(v5[:, b % 4, :, 3 * DH:3 * DH + 1], pw[:, b, 1:2].unsqueeze(1).to_broadcast([P, NH, 1]))\
                    .then_inc(v_ready, 1)
                dve.wait_ge(v_two, b + 1)
                dve.wait_ge(v_res, b + 1)
                dve.tensor_tensor(v5[:, b % 4, :, 2 * DH:3 * DH], vr[:, r], v5[:, b % 4, :, DH:2 * DH],
                                  ALU.subtract).then_inc(v_ready, 1)

            def q_columns(b):
                dve.wait_ge(T_full, T_AT["q", b])
                if b >= 4:
                    dve.wait_ge(qk_ok, (b - 3) * 4)
                dve.tensor_copy(qT[:, b % 4].rearrange("p j s -> p (j s)"), pT16).then_inc(qT_ok, 1)
                dve.wait_ge(qT_ok, b + 1)
                dve.sem_inc(T_free, 1)

            def gates(b):
                g, r = b // 2, b % 2
                dve.wait_ge(M_full, M_AT["gates", b])
                link(dve.tensor_reduce(gred[:, r], pM[:, 0:192].rearrange("p (a s i) -> p a i s", a=2, s=3),
                                       AX.X, ALU.add))
                dve.sem_inc(M_free, 1)
                link(dve.scalar_tensor_tensor(out=gt1[:, r, :], in0=gred[:, r, 1, :], scalar=pw[:, b, 1:2],
                                              in1=bias_sb[:, :], op0=ALU.mult, op1=ALU.add))
                if g >= 2 and r == 0:
                    dve.wait_ge(M_full, M_AT["gT", g - 2])
                dve.scalar_tensor_tensor(out=g_tm[:, g % 2, :, r, :],
                                         in0=gred[:, r, 0, :].rearrange("p (a h) -> p a h", a=2),
                                         scalar=1.0 / QSCALE, in1=gt1[:, r, :].rearrange("p (a h) -> p a h", a=2),
                                         op0=ALU.mult, op1=ALU.add).then_inc(gates_ok, 1)

            def gate_rows(g):
                dve.wait_ge(M_full, M_AT["gT", g])
                dve.tensor_copy(gT[:, :, :], pM[0:GB * NH, 0:2 * S].rearrange("p (a s) -> p a s", a=2))\
                    .then_inc(gT_ok, 1)
                dve.wait_ge(gT_ok, g + 1)
                dve.sem_inc(M_free, 1)

            def gate_scans(g):
                dve.wait_ge(gln_ok, g + 1)
                dve.wait_ge(pool_const, 2)
                link(dve.scalar_tensor_tensor(out=lf[:, 0, :], in0=gT[:, 1, :], scalar=0.0, in1=gabs[:, 2, :],
                                              op0=ALU.min, op1=ALU.subtract))
                link(dve.tensor_tensor_scan(lf[:, 1, :], ones[:, :], lf[:, 0, :], 0.0, ALU.mult, ALU.add))
                if g >= 1:
                    dve.wait_ge(M_full, M_AT["aT", g - 1])
                if g >= 2:
                    dve.wait_ge(g_row_in[g % 2], 16 * (g // 2))
                link(dve.tensor_tensor(aM[:, 0, :], gT[:, 0, :], lf[:, 1, :], ALU.subtract))
                link(dve.tensor_tensor_scan(Gm[:, g % 2, :], aM[:, 0, :], aM[:, 0, :], -3e38, ALU.max, ALU.max))
                dve.tensor_tensor(aM[:, 1, :], lf[:, 1, :], Gm[:, g % 2, :], ALU.add).then_inc(aM_ok, 1)

            def scores(n):
                dve.wait_ge(D_ok, n + 1)
                z = Z[:, n % 3].rearrange("p (j e) s -> p j e s", e=2)
                for e in range(2):
                    dve.wait_ge(qk_ok, 2 * n + e + 1)
                    dve.scalar_tensor_tensor(out=z[:, :, e, :], in0=pQK[e][:, :].rearrange("p (j s) -> p j s", s=S),
                                             scalar=CSCALE, in1=z[:, :, e, :], op0=ALU.mult, op1=ALU.mult)\
                        .then_inc(C_ok, 1)

            def low_scores(n):
                dve.wait_ge(Chi_ok, n + 1)
                dve.wait_ge(C_ok, 2 * n + 2)
                if n >= 2:
                    dve.wait_ge(pv_ok, n - 1)
                dve.tensor_tensor(Clo[:, n % 2], Z[:, n % 3], Chi[:, n % 2], ALU.subtract).then_inc(Clo_ok, 1)

            def head_sums(n):
                dve.wait_ge(pv_ok, n + 1)
                r, h0 = (n // 2) % 2, (n % 2) * UH
                pv = pPV[:, :].rearrange("p (h w) -> p h w", w=64)
                link(dve.tensor_reduce(U[:, r, h0:h0 + UH, :],
                                       pv[:, :, 0:3 * DH].rearrange("p h (s i) -> p h i s", s=3), AX.X, ALU.add))
                dve.tensor_copy(rs[:, r, h0:h0 + UH], pv[:, :, 3 * DH]).then_inc(pv_used, 1)
                dve.wait_ge(pv_used, n + 1)

            def out_norm(b):
                g, r = b // 2, b % 2
                e = eM[:, g % 2, r * NH:(r + 1) * NH]
                dve.wait_ge(a_ok, g + 1)
                dve.wait_ge(M_free, M_AT["aT", g])
                link(dve.scalar_tensor_tensor(out=nrm[:, r, 0, :], in0=rs[:, r, :], scalar=-1.0, in1=rs[:, r, :],
                                              op0=ALU.mult, op1=ALU.max))
                link(dve.scalar_tensor_tensor(out=nrm[:, r, 1, :], in0=e, scalar=OUTSCALE, in1=nrm[:, r, 0, :],
                                              op0=ALU.mult, op1=ALU.max))
                link(dve.tensor_scalar(nrm[:, r, 2, :], nrm[:, r, 1, :], OUTSCALE * EPS, None, ALU.add))
                link(dve.reciprocal(nrm[:, r, 3, :], nrm[:, r, 2, :]))
                link(dve.tensor_tensor(hh[:, r], U[:, r], bc(nrm[:, r, 3, :], DH), ALU.mult))
                link(dve.tensor_reduce(hst[:, r, 0, :], hh[:, r], AX.X, ALU.add))
                link(dve.scalar_tensor_tensor(out=hm[:, r], in0=bc(hst[:, r, 0, :], DH), scalar=-1.0 / DH,
                                              in1=hh[:, r], op0=ALU.mult, op1=ALU.add))
                link(dve.tensor_tensor(hsq[:, r], hm[:, r], hm[:, r], ALU.mult))
                dve.tensor_reduce(hst[:, r, 1, :], hsq[:, r], AX.X, ALU.add).then_inc(mean_var, 1)
                stats[0] += 1
                dve.wait_ge(mean_var, stats[0])
                dve.wait_ge(rstd_ok, stats[0])
                link(dve.tensor_tensor(hh[:, r], hm[:, r], bc(hst[:, r, 1, :], DH), ALU.mult))
                dve.wait_ge(in_late, 64)
                h = hh[:, r].rearrange("p h i -> p (h i)")
                link(dve.tensor_tensor(h, h, lnsc[:, :], ALU.mult))
                link(dve.tensor_tensor(x1[:, b, :], x_sb[:, b, :], h, ALU.add))
                row_stats(B + b, x1[:, b, :])
                if b >= 2:
                    dve.wait_ge(T_full, T_AT["x2", b - 2])
                dve.tensor_scalar(x2[:, r, :], x1[:, b, :], mv[:, B + b, 0:1], rstd[:, B + b, 0:1],
                                  ALU.subtract, ALU.mult).then_inc(x2_ok, 1)

            def logits(b):
                dve.wait_ge(M_full, M_AT["logits", b])
                dve.tensor_copy(lg[:, (b // 2) % 2, b % 2, :], pM[:, 0:NEX + 1]).then_inc(lg_ok, 1)
                dve.wait_ge(lg_ok, b + 1)
                dve.sem_inc(M_free, 1)

            def route(g):
                r = g % 2
                l = lg[:, r, :, 0:NEX]
                dve.tensor_reduce(nmx[:, r, :], l, AX.X, ALU.max, negate=True).then_inc(nmx_ok, 1)
                for b in range(GB):
                    lj = l[:, b, :].unsqueeze(1).to_broadcast([P, NEX, NEX])
                    le = l[:, b, :].unsqueeze(2).to_broadcast([P, NEX, NEX])
                    gt, eq, beat = (cmpt[:, r, i, b, :].rearrange("p (e j) -> p e j", j=NEX) for i in range(3))
                    link(dve.tensor_tensor(gt, lj, le, ALU.is_gt))
                    link(dve.tensor_tensor(eq, lj, le, ALU.is_equal))
                    link(dve.tensor_tensor(eq, eq, low[:, :, :], ALU.mult))
                    link(dve.tensor_tensor(beat, gt, eq, ALU.add))
                    link(dve.tensor_reduce(rank[:, r, 0, b, :], beat, AX.X, ALU.add))
                dve.wait_ge(ex_ok, 2 * GB * (g + 1))
                link(dve.tensor_scalar(esum[:, r, :, 1], ex[:, r, :, NEX], 1.0, None, ALU.add))
                link(dve.reciprocal(rcp[:, r], esum[:, r]))
                for b in range(GB):
                    link(dve.scalar_tensor_tensor(out=rank[:, r, 1, b, :], in0=rank[:, r, 0, b, :], scalar=2.0,
                                                  in1=ex[:, r, b, 0:NEX], op0=ALU.is_lt, op1=ALU.mult))
                    link(dve.tensor_scalar(rank[:, r, 0, b, :], rank[:, r, 1, b, :], rcp[:, r, b, 0:1], WSCALE,
                                           ALU.mult, ALU.mult))
                link(dve.tensor_copy(c16[:, r, :, 0, :], rank[:, r, 0]))
                dve.tensor_tensor(c16[:, r, :, 1, :], rank[:, r, 0], c16[:, r, :, 0, :], ALU.subtract)\
                    .then_inc(c16_ok, 1)

            def route_columns(g):
                dve.wait_ge(T_full, T_AT["cT", g])
                dve.tensor_copy(cT[:, g % 2, :], pT16[0:2 * NEX, 0:TOK]).then_inc(cT_ok, 1)
                dve.wait_ge(cT_ok, g + 1)
                dve.sem_inc(T_free, 1)

            def features(g, c):
                n = SLOTS * g + c
                m = rows(c)
                up2 = pU[n % 2][0:m, TOK:2 * TOK]
                dve.wait_ge(s_ok, n + 1)
                if n >= 3:
                    dve.wait_ge(dn_used, n - 2)
                if c < NC_SH:
                    dve.tensor_tensor(h_ff[0:m, n % 3, :], s_ff[0:m, n % 2, :], up2, ALU.mult).then_inc(h_ok, 1)
                    return
                e = (c - NC_SH) % 2
                dve.wait_ge(T_full, T_AT["cw", g, c - e])
                link(dve.scalar_tensor_tensor(out=p_ff[:, n % 2, :], in0=pT[:, e * TOK:(e + 1) * TOK],
                                              scalar=1.0 / WSCALE, in1=s_ff[:, n % 2, :], op0=ALU.mult, op1=ALU.mult))
                if e == 1 or c == SLOTS - 1:
                    dve.sem_inc(T_free, 1)
                dve.tensor_tensor(h_ff[:, n % 3, :], p_ff[:, n % 2, :], up2, ALU.mult).then_inc(h_ok, 1)

            def shared_out(g):
                dve.wait_ge(dn_used, SLOTS * g + NC_SH)
                for b in range(GB):
                    n = GB * g + b
                    dve.scalar_tensor_tensor(out=y_sb[:, n, :], in0=pD[:, b * E:(b + 1) * E],
                                             scalar=rcp[:, g % 2, b, 1:2], in1=x1[:, n, :],
                                             op0=ALU.mult, op1=ALU.add).then_inc(y_ok, 1)

            def final_out(g):
                dve.wait_ge(dn_used, SLOTS * (g + 1))
                dve.wait_ge(y_ok, GB * (g + 1))
                for b in range(GB):
                    n = GB * g + b
                    dve.tensor_tensor(o_sb[:, n, :], y_sb[:, n, :], pD[:, b * E:(b + 1) * E], ALU.add)\
                        .then_inc(o_ok, 1)

            gate_weights()
            for it in range(NG + 1):
                for k in range(SLOTS):
                    if it > 0:
                        if k == 2 and it > 1:
                            final_out(it - 2)
                    if it < NG:
                        if k < GB:
                            operands(GB * it + k)
                        if 1 <= k < 1 + GB:
                            q_columns(GB * it + k - 1)
                        if 2 <= k < 2 + GB:
                            gates(GB * it + k - 2)
                        if k == 4:
                            gate_rows(it)
                            gate_scans(it)
                        for u in range(UNITS):
                            if k == UNIT_SLOT[u]:
                                scores(UNITS * it + u)
                            if k == UNIT_SLOT[u] + 1:
                                low_scores(UNITS * it + u)
                                head_sums(UNITS * it + u)
                        for b in range(GB):
                            if k == N_SLOT[b]:
                                out_norm(GB * it + b)
                    if it > 0:
                        if k == 0:
                            for b in range(GB):
                                logits(GB * (it - 1) + b)
                        if k == R_SLOT:
                            route(it - 1)
                        if k == R_SLOT + 1:
                            route_columns(it - 1)
                        features(it - 1, k)
                        if k == NC_SH + 1:
                            shared_out(it - 1)
            final_out(NG - 1)

        @block.tensor
        def _(pe):
            def fill_T(key):
                if T_AT[key] > 1:
                    pe.wait_ge(T_free, T_AT[key] - 1)

            def fill_M(key):
                if M_AT[key] > 1:
                    pe.wait_ge(M_free, M_AT[key] - 1)

            def columns(b):
                r = b % 2
                pe.wait_ge(q_ready, b + 1)
                fill_T(("q", b))
                for j in range(NPAIR):
                    last = pe.transpose(pT16[:, j * S:(j + 1) * S],
                                        q3[:, r, 2 * j:2 * j + 2].rearrange("p h s i -> p (h s i)"), id16[:, :])
                last.then_inc(T_full, 1)
                pe.wait_ge(k_ready, b + 1)
                fill_T(("k", b))
                for j in range(NPAIR):
                    last = pe.transpose(pT16[:, j * S:(j + 1) * S],
                                        k3[:, r, 2 * j:2 * j + 2].rearrange("p h s i -> p (h s i)"), id16[:, :])
                last.then_inc(T_full, 1)

            def gates(b):
                fill_M(("gates", b))
                pe.wait_ge(qT_ok, b + 1)
                pe.wait_ge(kT_ok, b + 1)
                for w, operand in enumerate((qT, kT)):
                    for j in range(NPAIR):
                        last = pe.matmul(pM[:, 96 * w:96 * w + 96], operand[:, b % 4, j, :],
                                         wg_sb[:, w, j].rearrange("p s n -> p (s n)"),
                                         start=(j == 0), stop=(j == NPAIR - 1))
                last.then_inc(M_full, 1)

            def gate_rows(g):
                fill_M(("gT", g))
                pe.wait_ge(gates_ok, GB * (g + 1))
                for a in range(2):
                    last = pe.transpose(pM[0:GB * NH, a * S:(a + 1) * S],
                                        g_tm[:, g % 2, a].rearrange("p b h -> p (b h)"), id32[:, :])
                last.then_inc(M_full, 1)

            def gate_columns(g):
                fill_M(("aT", g))
                pe.wait_ge(aM_ok, g + 1)
                for a in range(2):
                    last = pe.transpose(pM[:, 64 * a:64 * a + GB * NH], aM[:, a, :], id32[0:GB * NH, 0:GB * NH])
                last.then_inc(M_full, 1)

            def scores(n):
                b, h0 = n // 2, (n % 2) * UH
                for e in range(2):
                    if n >= 1:
                        pe.wait_ge(C_ok, 2 * (n - 1) + e + 1)
                    for i in range(UH // 2):
                        j, base = (h0 + 2 * i) // 2, 64 * e
                        last = pe.matmul(pQK[e][:, i * S:(i + 1) * S], kT[base:base + 3 * DH, b % 4, j, :],
                                         qT[base:base + 3 * DH, b % 4, j, :], start=True, stop=True)
                    last.then_inc(qk_ok, 1)

            def outputs(n):
                b, h0 = n // 2, (n % 2) * UH
                pe.wait_ge(Clo_ok, n + 1)
                pe.wait_ge(Chi_ok, n + 1)
                if n % 2 == 0:
                    pe.wait_ge(v_ready, 2 * (b + 1))
                if n >= 1:
                    pe.wait_ge(pv_used, n)
                for i in range(UH):
                    o = pPV[:, 64 * i:64 * i + 3 * DH + 1]
                    v = v5[:, b % 4, h0 + i, 0:3 * DH + 1]
                    pe.matmul(o, Chi[:, n % 2, i, :], v, start=True, stop=False)
                    last = pe.matmul(o, Clo[:, n % 2, i, :], v, start=False, stop=True)
                last.then_inc(pv_ok, 1)

            def x2_columns(b):
                fill_T(("x2", b))
                pe.wait_ge(x2_ok, b + 1)
                for kk in range(2):
                    last = pe.transpose(pT[:, kk * S:(kk + 1) * S], x2[:, b % 2, kk * P:(kk + 1) * P], id32[:, :])
                last.then_inc(T_full, 1)

            def logits(b):
                fill_M(("logits", b))
                pe.wait_ge(x2T_ok, b + 1)
                for kk in range(2):
                    last = pe.matmul(pM[:, 0:NEX + 1], x2T[:, (b // 2) % 2, kk, (b % 2) * S:(b % 2 + 1) * S],
                                     gw[:, kk, :], start=(kk == 0), stop=(kk == 1))
                last.then_inc(M_full, 1)

            def route_columns(g):
                fill_T(("cT", g))
                pe.wait_ge(c16_ok, g + 1)
                for b in range(GB):
                    last = pe.transpose(pT16[0:2 * NEX, b * S:(b + 1) * S],
                                        c16[:, g % 2, b].rearrange("p s e -> p (s e)"), id16[:, :])
                last.then_inc(T_full, 1)

            def expert_up(g, c):
                n = SLOTS * g + c
                m = rows(c)
                if c == 0:
                    pe.wait_ge(x2T_ok, GB * (g + 1))
                if g == 0:
                    pe.wait_ge(in_up[c], 16)
                if n >= 2:
                    pe.wait_ge(h_ok, n - 1)
                for w in range(2):
                    for kk in range(2):
                        last = pe.matmul(pU[n % 2][0:m, w * TOK:(w + 1) * TOK], w_up[:, c, w, kk, 0:m],
                                         x2T[:, g % 2, kk, :], start=(kk == 0), stop=(kk == 1))
                last.then_inc(up_ok, 1)

            def weight_rows(g, c):
                fill_T(("cw", g, c))
                pe.wait_ge(cT_ok, g + 1)
                for e in range(min(2, SLOTS - c)):
                    f = c - NC_SH + e
                    last = pe.matmul(pT[:, e * TOK:(e + 1) * TOK], sel[:, f * P:(f + 1) * P], cT[:, g % 2, :],
                                     start=True, stop=True)
                last.then_inc(T_full, 1)

            def expert_down(g, c):
                n = SLOTS * g + c
                m = rows(c)
                if g == 0 and c % 6 == 0 and c < 18:
                    pe.wait_ge(in_dn[dn_part(c)], 16)
                if c == 0 and g > 0:
                    pe.wait_ge(o_ok, GB * g)
                if c == NC_SH:
                    pe.wait_ge(y_ok, GB * (g + 1))
                pe.wait_ge(h_ok, n + 1)
                for b in range(GB):
                    first = b == 0 and c in (0, NC_SH)
                    last = pe.matmul(pD[:, b * E:(b + 1) * E], h_ff[0:m, n % 3, b * S:(b + 1) * S],
                                     w_dn[0:m, c, :], start=first, stop=c in (NC_SH - 1, SLOTS - 1),
                                     skip_group_check=True)
                last.then_inc(dn_used, 1)

            pe.wait_ge(in_const, 32)
            pe.wait_ge(pool_const, 6)
            pe.wait_ge(wg_part, 1)
            for it in range(NG + 1):
                for k in range(SLOTS):
                    if it > 1 and k < 2:
                        expert_down(it - 2, SLOTS - 2 + k)
                    if it < NG:
                        if 1 <= k < 1 + GB:
                            columns(GB * it + k - 1)
                        if 2 <= k < 2 + GB:
                            gates(GB * it + k - 2)
                        if k == 4:
                            gate_rows(it)
                        if k == 5:
                            gate_columns(it)
                        for u in range(UNITS):
                            if k == UNIT_SLOT[u]:
                                scores(UNITS * it + u)
                            if k == UNIT_SLOT[u] + 1:
                                outputs(UNITS * it + u)
                        for b in range(GB):
                            if k == X2_SLOT[b]:
                                x2_columns(GB * it + b)
                    if it > 0:
                        if k == 0:
                            for b in range(GB):
                                logits(GB * (it - 1) + b)
                        if k == R_SLOT + 1:
                            route_columns(it - 1)
                        expert_up(it - 1, k)
                        if k >= NC_SH and (k - NC_SH) % 2 == 0:
                            weight_rows(it - 1, k)
                        if k >= 2:
                            expert_down(it - 1, k - 2)
            expert_down(NG - 1, SLOTS - 2)
            expert_down(NG - 1, SLOTS - 1)


def constants():
    ident = np.eye(P, dtype=np.float32)
    expert = np.arange(NC_EX * P) // FM
    select = (np.arange(2 * NEX)[:, None] % NEX == expert[None, :]).astype(np.float16)
    lower = np.broadcast_to(np.tril(np.ones((NEX, NEX), np.float32), -1), (P, NEX, NEX))
    return {"ident": ident, "ident16": ident.astype(np.float16), "select": select,
            "lower": np.ascontiguousarray(lower)}


def layouts(a):
    out = {"x": a["x"], "ctx_in": a["ctx_2048"]}
    gates = np.concatenate([a["L0_xattn_Wi"], a["L0_xattn_Wf"]], axis=1)
    gates = gates.reshape(3, NPAIR, 2, DH, 2 * NH).transpose(0, 2, 3, 1, 4)
    wg = np.zeros((2, 4, DH, 3, NPAIR, 2 * NH), np.float32)
    for slot in (0, 2):
        wg[:, slot, :, 0] = gates[0]
    for w in (1, 2):
        for slot in (0, 1):
            wg[:, slot, :, w] = gates[w]
    out["wg"] = wg.reshape(P, 3, NPAIR * 2 * NH)
    out["bias_g"] = np.concatenate([a["L0_xattn_bi"], a["L0_xattn_bf"]])
    out["ln_scale"] = a["L0_xattn_ln_scale"]
    route = np.concatenate([a["L0_ffn_gate_w"], a["L0_ffn_shared_gate_w"]], axis=0)
    out["gate_w"] = route.T.reshape(2, P, NEX + 1).transpose(1, 0, 2)
    up = np.zeros((2, SLOTS * P, E), np.float32)
    for w in range(2):
        up[w, 0:FS] = a[f"L0_ffn_shared_fc{w + 1}"]
        up[w, NC_SH * P:] = a[f"L0_ffn_expert_fc{w + 1}"].reshape(NEX * FM, E)
    out["up"] = up.reshape(2, SLOTS, P, 2, P).transpose(1, 4, 0, 3, 2)
    down = np.zeros((SLOTS * P, E), np.float32)
    down[0:FS] = a["L0_ffn_shared_proj"].T
    down[NC_SH * P:] = a["L0_ffn_expert_proj"].transpose(0, 2, 1).reshape(NEX * FM, E)
    out["down"] = down.reshape(SLOTS, P, E).transpose(1, 0, 2)
    return {k: np.ascontiguousarray(v) for k, v in out.items()}


def kernel(**inputs):
    import concourse.bacc as bacc
    from concourse.bass_utils import run_bass_kernel_spmd

    arrays = layouts({k: np.asarray(v) for k, v in inputs.items()}) | constants()
    nc = bacc.Bacc("TRN2", target_bir_lowering=False, num_devices=1)
    args = {k: nc.dram_tensor(k, v.shape, mybir.dt.from_np(v.dtype), kind="ExternalInput").ap()
            for k, v in arrays.items()}
    out = nc.dram_tensor("out", (B, S, E), F32, kind="ExternalOutput").ap()
    build(nc, **args, out=out)
    r = run_bass_kernel_spmd(nc, [arrays], core_ids=[0])
    return r.results[0]["out"]
```

```python
from contextlib import ExitStack

import concourse.bass as bass
from concourse import mybir
import numpy as np

F32, F16, BF16, I32 = mybir.dt.float32, mybir.dt.float16, mybir.dt.bfloat16, mybir.dt.int32
ALU, ACT, AX = mybir.AluOpType, mybir.ActivationFunctionType, mybir.AxisListType
MAX = bass.bass_isa.ReduceOp.max

P = 128
B, S, E = 8, 128, 256
NH = 16
DH = E // NH
NEX, FM, FS = 8, 176, 704
GB = 2
NG = B // GB
TOK = GB * S
NPAIR = NH // 2
NC_SH = -(-FS // P)
NC_EX = NEX * FM // P
SLOTS = NC_SH + NC_EX
REST = FS - (NC_SH - 1) * P
UH = 8
UNITS = GB * NH // UH
UW = UH * S
LN_EPS, EPS = 1e-5, 1e-6
FAR = 1e30
QSCALE = 2.0 ** 11
KSCALE = 2.0 ** 13
CSCALE = 2.0 ** -16
RSUM = 1 / (QSCALE * CSCALE * DH ** 0.5)
MSCALE = 2.0 ** 14
UPSCALE = QSCALE * MSCALE
WSCALE = 2.0 ** 15
PIECES = 4

STATS = 0
SCALES = 2
HIGHS = 3
LOWS = 5
K_COLS, Q_COLS = [7, 9], [8, 10]
GATES = [11, 13]
GATE_ROWS = 15
SCANS = 18
GATE_COLS = 20
BROADCAST = 19
UNIT = 3
SCORES = 22
NORM = [31, 37]
X2_COLS = [40, 46]
LOGITS = 48
ROUTE_COLS = 52
SPREAD = [54, 58, 61]
FFN = 48
SPREAD_CHUNKS = 4
END = (NG - 1) * SLOTS + FFN + SLOTS + 4


def rows(c):
    return REST if c == NC_SH - 1 else P


def group_at(t, offset):
    g, late = divmod(t - offset, SLOTS)
    return g if late == 0 and 0 <= g < NG else None


def chunk_at(t, lag):
    n = t - FFN - lag
    return n if 0 <= n < NG * SLOTS else None


def fills(steps):
    order = sorted((SLOTS * g + slot, name, n(g)) for name, slot, n in steps for g in range(NG))
    keys = [key[1:] for key in order]
    return dict(zip(keys, [None] + keys)), {key: i + 1 for i, key in enumerate(keys)}


def row(b):
    return lambda g: GB * g + b


def group(g):
    return g


T_BEFORE, T_AT = fills([("k", K_COLS[0], row(0)), ("k", K_COLS[1], row(1)), ("gates", GATES[0], row(0)),
                        ("gates", GATES[1], row(1)), ("gT", GATE_ROWS, group), ("x2", X2_COLS[0], row(0))])
M_BEFORE, M_AT = fills([("q", Q_COLS[0], row(0)), ("q", Q_COLS[1], row(1)), ("aT", GATE_COLS, group),
                        ("x2", X2_COLS[1], row(1)), ("logits", LOGITS, group), ("cT", ROUTE_COLS, group)])


def build(nc, x, ctx_in, wg, bias_g, ln_scale, gate_w, up, down, ident, ident16, select, lower, out):
    with ExitStack() as stack:
        def sb(name, shape, dt=F32):
            return stack.enter_context(nc.sbuf_tensor(name, shape, dt))

        def sem(name):
            return stack.enter_context(nc.semaphore(name))

        def bank(name):
            return stack.enter_context(nc.psum_tensor(name, [P, 512], F32))

        x_sb = sb("x_sb", [P, B, E])
        ctx_sb = sb("ctx_sb", [P, B, E])
        id32 = sb("id32", [P, P])
        id16 = sb("id16", [P, P], F16)
        sel = sb("sel", [2 * NEX, NC_EX * P], F16)
        low = sb("low", [P, NEX, NEX])
        bias_sb = sb("bias_sb", [P, 2 * NH])
        lnsc = sb("lnsc", [P, E])
        gw = sb("gw", [P, 2, NEX + 1])
        gwr = sb("gwr", [P, 2, NEX + 1])
        gw3 = sb("gw3", [P, 2, 3, NEX + 1], BF16)
        wg_in = sb("wg_in", [P, 3, NPAIR * 2 * NH])
        wg_sb = sb("wg_sb", [P, 2, NPAIR, 3, 2 * NH], BF16)
        wg_r = sb("wg_r", [P, 2, NPAIR, 2 * NH])
        w_up = sb("w_up", [P, SLOTS, 2, 2, P])
        up16 = sb("up16", [P, SLOTS, 2, 2, 2, P], F16)
        w_dn = sb("w_dn", [P, SLOTS, E])
        wmax = sb("wmax", [P, 2, PIECES])
        wall = sb("wall", [P, 2, PIECES])
        wpow = sb("wpow", [P, 2, 2])
        wmul = sb("wmul", [P, 2])
        unscale = sb("unscale", [P, 2, 3])
        half = sb("half", [P, NH])
        ones = sb("ones", [GB * NH, S])

        st6 = sb("st6", [P, 2 * B, 6])
        mv = sb("mv", [P, 2 * B, 2])
        ve = sb("ve", [P, 2 * B])
        rstd = sb("rstd", [P, 2 * B])
        nb = sb("nb", [P, 2 * B])
        kmax = sb("kmax", [P, NG])
        kall = sb("kall", [P, NG])
        kpow = sb("kpow", [P, NG, 6])
        qs = sb("qs", [P, 2, E])
        q3 = sb("q3", [P, 2, NH, 4, DH], F16)
        k3 = sb("k3", [P, 4, NH, 4, DH], F16)
        qT = sb("qT", [P, 4, NPAIR, S], F16)
        kT = sb("kT", [P, 4, NPAIR, S], F16)
        gred = sb("gred", [P, 2, 2, 2 * NH])
        gt1 = sb("gt1", [P, 2, 2 * NH])
        g_tm = sb("g_tm", [P, 2, 2, GB, NH])
        gT = sb("gT", [GB * NH, 2, S])
        gabs = sb("gabs", [GB * NH, 3, S])
        lf = sb("lf", [GB * NH, 2, S])
        aM = sb("aM", [GB * NH, 2, S])
        Gm = sb("Gm", [GB * NH, 2, S])
        Grow = sb("Grow", [1, GB * NH * S])
        a_tm = sb("a_tm", [P, 2, GB * NH])
        eM = sb("eM", [P, 2, GB * NH])
        Z = sb("Z", [P, 3, UH, S])
        Chi = sb("Chi", [P, 2, UH, S], F16)
        Clo = sb("Clo", [P, 2, UH, S], F16)
        U = sb("U", [P, 2, NH, DH])
        rs = sb("rs", [P, 2, NH])
        nrm = sb("nrm", [P, 2, 5, NH])
        hh = sb("hh", [P, NH, DH])
        hm = sb("hm", [P, 2, NH, DH])
        hsq = sb("hsq", [P, 2, NH, DH])
        hst = sb("hst", [P, 2, 4, NH])
        x1 = x_sb
        x2hl = sb("x2hl", [P, 2, 2, E], F16)

        lgs = sb("lgs", [P, 2, GB, NEX + 1])
        lg = sb("lg", [P, 2, GB, NEX + 1])
        nmx = sb("nmx", [P, 2, GB])
        ex = sb("ex", [P, 2, GB, NEX + 1])
        esum = sb("esum", [P, 2, GB, 2])
        rcp = sb("rcp", [P, 2, GB, 2])
        cmpt = sb("cmpt", [P, 3, GB, NEX * NEX])
        rank = sb("rank", [P, 2, 2, GB, NEX])
        c16 = sb("c16", [P, 2, GB, 2, NEX], F16)
        early = w_up[:, 0:NC_SH].rearrange("p c w k f -> p (c w k f)")
        x2 = early[:, 0:2 * E].rearrange("p (r e) -> p r e", r=2)
        h_ff = early[:, 512:1280].rearrange("p (r t) -> p r t", r=3)
        x2T = early[:, 1280:2304].bitcast(F16).rearrange("p (r a k t) -> p r a k t", r=2, a=2, k=2)
        cT = early[0:2 * NEX, 2304:2560].bitcast(F16).rearrange("p (r t) -> p r t", r=2)
        late = w_up[:, NC_SH:].rearrange("p c w k f -> p (c w k f)")
        cw = late[:, 0:NC_EX * TOK].rearrange("p (f t) -> p f t", f=NC_EX)
        s_ff = wg_in[:, 0:2, :]
        p_ff = wg_r[:, :, :, :].rearrange("p w j n -> p w (j n)")
        y_sb, o_sb = x_sb, ctx_sb

        pT = bank("pT")
        pM = bank("pM")
        pT16, pM16 = pT[:, :].bitcast(F16), pM[:, :].bitcast(F16)
        pQK = [bank("pQK0"), bank("pQK1")]
        pPV = bank("pPV")
        pU = [bank("pU0"), bank("pU1")]
        pD = bank("pD")

        in_rows = [sem(f"in_rows{b}") for b in range(B)]
        in_const, in_wg, in_late = sem("in_const"), sem("in_wg"), sem("in_late")
        in_up = [[sem(f"in_up{p}_{i}") for i in range(PIECES)] for p in range(2)]
        in_dn = [sem(f"in_dn{p}") for p in range(2)]
        g_row_in, stored = sem("g_row_in"), sem("stored")
        dve_step, act_step, pool_step = sem("dve_step"), sem("act_step"), sem("pool_step")
        pool_const, wg_part, gw_ok = sem("pool_const"), sem("wg_part"), sem("gw_ok")
        wmax_ok, wall_ok, wmul_ok = sem("wmax_ok"), sem("wall_ok"), sem("wmul_ok")
        whi_ok, wlo_ok = sem("whi_ok"), sem("wlo_ok")
        stats_ok = sem("stats_ok")
        rstd_ok = sem("rstd_ok")
        scales_ok = sem("scales_ok")
        q_hi, k_hi, q_low, k_low = sem("q_hi"), sem("k_hi"), sem("q_low"), sem("k_low")
        T_full, M_full = sem("T_full"), sem("M_full")
        qT_ok, kT_ok = sem("qT_ok"), sem("kT_ok")
        gsum_ok, gates_ok, gT_ok, gln_ok, aM_ok = sem("gsum_ok"), sem("gates_ok"), sem("gT_ok"), sem("gln_ok"), sem("aM_ok")
        a_ok, eM_ok, z_ok, D_ok = sem("a_ok"), sem("eM_ok"), sem("z_ok"), sem("D_ok")
        qk_ok, C_ok, Chi_ok, Clo_ok, pv_ok, pv_used = (sem("qk_ok"), sem("C_ok"), sem("Chi_ok"), sem("Clo_ok"),
                                                       sem("pv_ok"), sem("pv_used"))
        hm_ok, hsq_ok, hvar_ok, ho_ok = sem("hm_ok"), sem("hsq_ok"), sem("hvar_ok"), sem("ho_ok")
        stats2_ok, rstd2_ok, nb2_ok = sem("stats2_ok"), sem("rstd2_ok"), sem("nb2_ok")
        x2_hi, x2_low, x2T_ok = sem("x2_hi"), sem("x2_low"), sem("x2T_ok")
        lgs_ok, nmx_ok, ex_ok, c16_ok, cT_ok = sem("lgs_ok"), sem("nmx_ok"), sem("ex_ok"), sem("c16_ok"), sem("cT_ok")
        spread_ok, cw_ok = sem("spread_ok"), sem("cw_ok")
        up_ok = sem("up_ok")
        s_ok, h_ok = sem("s_ok"), sem("h_ok")
        dn_used = sem("dn_used")
        y_ok, o_ok = sem("y_ok"), sem("o_ok")

        block = stack.enter_context(nc.Block())

        def bc(ap, n):
            return ap.unsqueeze(2).to_broadcast([ap.shape[0], ap.shape[1], n])

        def x2_bank(b):
            return (pT16, T_full, T_AT["x2", b]) if b % GB == 0 else (pM16, M_full, M_AT["x2", b])

        PART = [(0, NC_SH), (NC_SH, SLOTS)]

        def part(c):
            return int(c >= NC_SH)

        def piece(p, i):
            lo, hi = PART[p]
            return lo + (hi - lo) * i // PIECES, lo + (hi - lo) * (i + 1) // PIECES

        SIZES = [[9, 10, 10, 11], [12, 14, 16, 17]]
        ALL_MAX = [12, 21]
        WSCALES = [14, 23]
        SPLIT = 25

        @block.sync
        def _(sp):
            for b in range(GB):
                sp.dma_start(x_sb[:, b, :], x[b]).then_inc(in_rows[b], 16)
                sp.dma_start(ctx_sb[:, b, :], ctx_in[b]).then_inc(in_rows[b], 16)
            for p, (lo, hi) in enumerate(PART):
                for i in range(PIECES):
                    c0, c1 = piece(p, i)
                    sp.dma_start(w_up[:, c0:c1], up[c0:c1].rearrange("c p w k f -> p c w k f")).then_inc(in_up[p][i], 16)
                for b in (range(GB, 2 * GB), range(2 * GB, B))[p]:
                    sp.dma_start(x_sb[:, b, :], x[b]).then_inc(in_rows[b], 16)
                    sp.dma_start(ctx_sb[:, b, :], ctx_in[b]).then_inc(in_rows[b], 16)
                sp.dma_start(w_dn[:, lo:hi, :], down[:, lo:hi, :]).then_inc(in_dn[p], 16)
            for g in range(NG):
                sp.wait_ge(aM_ok, g + 1)
                if g >= 1:
                    sp.wait_ge(z_ok, UNITS * g)
                sp.dma_start(Grow[0:1, :], Gm[:, g % 2, :]).then_inc(g_row_in, 16)
            for b in range(B):
                sp.wait_ge(o_ok, b + 1)
                sp.dma_start(out[b], o_sb[:, b, :]).then_inc(stored, 16)
            sp.wait_ge(stored, 16 * B)

        @block.gpsimd
        def _(pool):
            steps = [0]

            def link(instruction):
                steps[0] += 1
                instruction.then_inc(pool_step, 1)
                pool.wait_ge(pool_step, steps[0])

            def row_deviations(g):
                n = slice(GB * g, GB * g + GB)
                pool.wait_ge(stats_ok, g + 1)
                link(pool.tensor_scalar(ve[:, n], mv[:, n, 1], LN_EPS, QSCALE ** -2, ALU.add, ALU.mult))
                pool.tensor_tensor(rstd[:, n], ve[:, n], half[:, 0:GB], ALU.pow).then_inc(rstd_ok, 1)
                pool.partition_all_reduce(kall[:, g:g + 1], kmax[:, g:g + 1], P, MAX).then_inc(rstd_ok, 1)

            def low_queries(g):
                for b in range(GB * g, GB * g + GB):
                    pool.wait_ge(q_hi, b + 1)
                    q = qs[:, b % 2, :].rearrange("p (h i) -> p h i", i=DH)
                    pool.tensor_tensor(q3[:, b % 2, :, 2, :], q, q3[:, b % 2, :, 0, :], ALU.subtract).then_inc(q_low, 1)

            def maxima(n):
                g, u = divmod(n, UNITS)
                if u == 0:
                    pool.wait_ge(g_row_in, 16 * (g + 1))
                if n >= 3:
                    pool.wait_ge(Clo_ok, n - 2)
                z = Z[:, n % 3]
                link(pool.partition_broadcast(z.rearrange("p h s -> p (h s)"), Grow[0:1, u * UW:(u + 1) * UW], P))
                pool.affine_select(out=z, in_=z, compare_op=ALU.is_ge, fill=FAR, base=0,
                                   pattern=[[0, UH], [1, S]], channel_multiplier=-1).then_inc(z_ok, 1)

            def low_scores(n):
                pool.wait_ge(Chi_ok, n + 1)
                if n >= 2:
                    pool.wait_ge(pv_ok, n - 1)
                pool.tensor_tensor(Clo[:, n % 2], Z[:, n % 3], Chi[:, n % 2], ALU.subtract).then_inc(Clo_ok, 1)

            def scaled_heads(b):
                r = b % 2
                pool.wait_ge(hvar_ok, b + 1)
                link(pool.tensor_scalar(hst[:, r, 2, :], hst[:, r, 1, :], 1.0 / DH, EPS, ALU.mult, ALU.add))
                link(pool.tensor_tensor(hst[:, r, 3, :], hst[:, r, 2, :], half[:, :], ALU.pow))
                link(pool.tensor_tensor(hsq[:, r], hm[:, r], bc(hst[:, r, 3, :], DH), ALU.mult))
                h = hsq[:, r].rearrange("p h i -> p (h i)")
                pool.tensor_tensor(h, h, lnsc[:, :], ALU.mult).then_inc(ho_ok, 1)

            def row_deviation2(b):
                n = slice(B + b, B + b + 1)
                pool.wait_ge(stats2_ok, b + 1)
                link(pool.tensor_scalar(ve[:, n], mv[:, n, 1], LN_EPS, QSCALE ** -2, ALU.add, ALU.mult))
                pool.tensor_tensor(rstd[:, n], ve[:, n], half[:, 0:1], ALU.pow).then_inc(rstd2_ok, 1)

            def low_rows(b):
                pool.wait_ge(x2_hi, b + 1)
                pool.tensor_tensor(x2hl[:, b % 2, 1, :], x2[:, b % 2, :], x2hl[:, b % 2, 0, :], ALU.subtract)\
                    .then_inc(x2_low, 1)

            def weight_max(p):
                pool.wait_ge(wmax_ok, PIECES * (p + 1))
                pool.partition_all_reduce(wall[:, p, :], wmax[:, p, :], P, MAX).then_inc(wall_ok, 1)

            pool.memset(half[:, :], -0.5).then_inc(pool_const, 1)
            pool.memset(ones[:, :], 1.0).then_inc(pool_const, 1)
            pool.memset(q3[:, :, :, 3, :], 0.0).then_inc(pool_const, 1)
            pool.memset(k3[:, :, :, 3, 1:DH], 0.0).then_inc(pool_const, 1)
            pool.memset(k3[:, :, :, 3, 0:1], 1.0).then_inc(pool_const, 1)
            pool.wait_ge(pool_const, 5)
            pool.wait_ge(in_late, 64)
            for t in range(END):
                if (g := group_at(t, STATS + 1)) is not None:
                    row_deviations(g)
                if (g := group_at(t, LOWS)) is not None:
                    low_queries(g)
                for u in range(UNITS):
                    if (g := group_at(t, SCORES + 3 + UNIT * u)) is not None:
                        low_scores(UNITS * g + u)
                for b in range(GB):
                    if (g := group_at(t, NORM[b] + 3)) is not None:
                        scaled_heads(GB * g + b)
                    if (g := group_at(t, NORM[b] + 5)) is not None:
                        row_deviation2(GB * g + b)
                    if (g := group_at(t, NORM[b] + 8)) is not None:
                        low_rows(GB * g + b)
                for u in range(UNITS):
                    if (g := group_at(t, BROADCAST + UNIT * u)) is not None:
                        maxima(UNITS * g + u)
                for p in range(2):
                    if t == ALL_MAX[p]:
                        weight_max(p)

        @block.scalar
        def _(act):
            steps = [0]

            def link(instruction):
                steps[0] += 1
                instruction.then_inc(act_step, 1)
                act.wait_ge(act_step, steps[0])

            act.dma_start(id32[:, :], ident).then_inc(in_const, 16)
            act.dma_start(id16[:, :], ident16).then_inc(in_const, 16)
            act.dma_start(wg_in[:, :, :], wg).then_inc(in_wg, 16)
            act.dma_start(bias_sb[:, :], bias_g.partition_broadcast(P)).then_inc(in_wg, 16)
            act.dma_start(lnsc[:, :], ln_scale.partition_broadcast(P)).then_inc(in_late, 16)
            act.dma_start(gw[:, :, :], gate_w).then_inc(in_late, 16)
            act.dma_start(sel[:, :], select).then_inc(in_late, 16)
            act.dma_start(low[:, :, :], lower).then_inc(in_late, 16)

            def high_keys(g):
                act.wait_ge(scales_ok, g + 1)
                for b in range(GB * g, GB * g + GB):
                    if b >= 2:
                        act.wait_ge(q_low, b - 1)
                    act.activation(qs[:, b % 2, :], x_sb[:, b, :], ACT.Identity, bias=nb[:, b:b + 1],
                                   scale=rstd[:, b:b + 1]).then_inc(act_step, 1)
                    steps[0] += 1
                for b in range(GB * g, GB * g + GB):
                    if b >= 4:
                        act.wait_ge(pv_ok, 2 * (b - 3))
                    c = ctx_sb[:, b, :].rearrange("p (h i) -> p h i", i=DH)
                    act.activation(k3[:, b % 4, :, 0:4:2, :], c.unsqueeze(2).to_broadcast([P, NH, 2, DH]), ACT.Copy,
                                   scale=kpow[:, g, 2:3]).then_inc(k_hi, 1)

            def high_queries(g):
                act.wait_ge(act_step, steps[0])
                for b in range(GB * g, GB * g + GB):
                    if b >= 2:
                        act.wait_ge(M_full, M_AT["q", b - 2])
                    q = qs[:, b % 2, :].rearrange("p (h i) -> p h i", i=DH)
                    act.activation(q3[:, b % 2, :, 0:2, :], q.unsqueeze(2).to_broadcast([P, NH, 2, DH]), ACT.Copy)\
                        .then_inc(q_hi, 1)

            def key_columns(b):
                act.wait_ge(T_full, T_AT["k", b])
                if b >= 4:
                    act.wait_ge(qk_ok, (b - 3) * 4)
                act.activation(kT[:, b % 4].rearrange("p j s -> p (j s)"), pT16, ACT.Copy).then_inc(kT_ok, 1)

            def query_columns(b):
                act.wait_ge(M_full, M_AT["q", b])
                if b >= 4:
                    act.wait_ge(qk_ok, (b - 3) * 4)
                act.activation(qT[:, b % 4].rearrange("p j s -> p (j s)"), pM16, ACT.Copy).then_inc(qT_ok, 1)

            def forget_logs(g):
                act.wait_ge(gT_ok, g + 1)
                link(act.activation(gabs[:, 0, :], gT[:, 1, :], ACT.Abs))
                link(act.activation(gabs[:, 1, :], gabs[:, 0, :], ACT.Exp, scale=-1.0))
                act.activation(gabs[:, 2, :], gabs[:, 1, :], ACT.Ln, bias=1.0).then_inc(gln_ok, 1)

            def gate_columns(g):
                act.wait_ge(M_full, M_AT["aT", g])
                if g >= 2:
                    act.wait_ge(hm_ok, GB * (g - 1))
                act.activation(a_tm[:, g % 2, :], pM[:, 0:GB * NH], ACT.Copy).then_inc(a_ok, 1)
                act.activation(eM[:, g % 2, :], pM[:, 64:64 + GB * NH], ACT.Exp, scale=-1.0).then_inc(eM_ok, 1)

            def decays(n):
                g, u = divmod(n, UNITS)
                act.wait_ge(z_ok, n + 1)
                act.wait_ge(a_ok, g + 1)
                for i in range(UH):
                    h = u * UH + i
                    last = act.activation(Z[:, n % 3, i, :], Z[:, n % 3, i, :], ACT.Exp,
                                          bias=a_tm[:, g % 2, h:h + 1], scale=-1.0)
                last.then_inc(D_ok, 1)

            def high_scores(n):
                act.wait_ge(C_ok, 2 * n + 2)
                if n >= 2:
                    act.wait_ge(pv_ok, n - 1)
                act.activation(Chi[:, n % 2], Z[:, n % 3], ACT.Copy).then_inc(Chi_ok, 1)

            def squares(b):
                act.wait_ge(hm_ok, b + 1)
                act.activation(hsq[:, b % 2], hm[:, b % 2], ACT.Square).then_inc(hsq_ok, 1)

            def high_rows(b):
                act.wait_ge(nb2_ok, b + 1)
                if b >= 2:
                    act.wait_ge(x2_low, b - 1)
                    act.wait_ge(*x2_bank(b - 2)[1:])
                link(act.activation(x2[:, b % 2, :], x1[:, b, :], ACT.Identity, bias=nb[:, B + b:B + b + 1],
                                    scale=rstd[:, B + b:B + b + 1]))
                act.activation(x2hl[:, b % 2, 0, :], x2[:, b % 2, :], ACT.Copy).then_inc(x2_hi, 1)

            def x2_columns(b):
                source, full, count = x2_bank(b)
                g = b // GB
                act.wait_ge(full, count)
                if g >= 2:
                    act.wait_ge(up_ok, SLOTS * (g - 1))
                o = x2T[:, g % 2, :, :, (b % 2) * S:(b % 2 + 1) * S].rearrange("p a k s -> p (a k) s")
                act.activation(o, source[:, 0:4 * S].rearrange("p (k s) -> p k s", k=4), ACT.Copy).then_inc(x2T_ok, 1)

            def route_exps(g):
                act.wait_ge(nmx_ok, g + 1)
                for b in range(GB):
                    act.activation(ex[:, g % 2, b, 0:NEX], lg[:, g % 2, b, 0:NEX], ACT.Exp,
                                   bias=nmx[:, g % 2, b:b + 1], accum_out=esum[:, g % 2, b, 0:1]).then_inc(ex_ok, 1)
                    act.activation(ex[:, g % 2, b, NEX:NEX + 1], lg[:, g % 2, b, NEX:NEX + 1], ACT.Exp,
                                   scale=-1.0).then_inc(ex_ok, 1)

            def route_columns(g):
                act.wait_ge(M_full, M_AT["cT", g])
                if g >= 2:
                    act.wait_ge(spread_ok, (NC_EX + 1) // 2 * (g - 1))
                act.activation(cT[:, g % 2, :], pM16[0:2 * NEX, 0:TOK], ACT.Copy).then_inc(cT_ok, 1)

            def spread_out(g, i):
                pairs = (NC_EX + 1) // 2
                for j in range(2 * i, 2 * i + 2):
                    f0, f1 = 2 * j, min(2 * j + 2, NC_EX)
                    act.wait_ge(spread_ok, pairs * g + j + 1)
                    if g >= 1:
                        act.wait_ge(h_ok, SLOTS * (g - 1) + NC_SH + f1)
                    act.activation(cw[:, f0:f1, :].rearrange("p f t -> p (f t)"), pQK[j % 2][:, 0:(f1 - f0) * TOK],
                                   ACT.Copy).then_inc(cw_ok, 1)

            def high_weights(c):
                p = part(c)
                act.wait_ge(wmul_ok, p + 1)
                act.activation(up16[:, c, 0], w_up[:, c], ACT.Copy, scale=wmul[:, p:p + 1]).then_inc(whi_ok, 1)

            def gate_tanh(n):
                c = n % SLOTS
                m = rows(c)
                act.wait_ge(up_ok, n + 1)
                if n >= 2:
                    act.wait_ge(h_ok, n - 1)
                act.activation(s_ff[0:m, n % 2, :], pU[n % 2][0:m, 0:TOK], ACT.Tanh,
                               scale=unscale[0:m, part(c), 0:1]).then_inc(s_ok, 1)

            for t in range(END):
                if (n := chunk_at(t, 1)) is not None:
                    gate_tanh(n)
                for i in range(len(SPREAD)):
                    if (g := group_at(t, SPREAD[i] + 1)) is not None:
                        spread_out(g, i)
                for b in range(GB):
                    if (g := group_at(t, X2_COLS[b] + 1)) is not None:
                        x2_columns(GB * g + b)
                    if (g := group_at(t, K_COLS[b] + 1)) is not None:
                        key_columns(GB * g + b)
                    if (g := group_at(t, Q_COLS[b] + 1)) is not None:
                        query_columns(GB * g + b)
                if (g := group_at(t, GATE_COLS + 1)) is not None:
                    gate_columns(g)
                if (g := group_at(t, LOGITS + 2)) is not None:
                    route_exps(g)
                if (g := group_at(t, ROUTE_COLS + 1)) is not None:
                    route_columns(g)
                for b in range(GB):
                    if (g := group_at(t, NORM[b] + 1)) is not None:
                        squares(GB * g + b)
                    if (g := group_at(t, NORM[b] + 7)) is not None:
                        high_rows(GB * g + b)
                if (g := group_at(t, GATE_ROWS + 2)) is not None:
                    forget_logs(g)
                for u in range(UNITS):
                    if (g := group_at(t, SCORES + 2 + UNIT * u)) is not None:
                        high_scores(UNITS * g + u)
                    if (g := group_at(t, SCORES + UNIT * u)) is not None:
                        decays(UNITS * g + u)
                if (g := group_at(t, HIGHS)) is not None:
                    high_keys(g)
                if (g := group_at(t, HIGHS + 1)) is not None:
                    high_queries(g)
                if SPLIT <= t < SPLIT + SLOTS:
                    high_weights(t - SPLIT)

        @block.vector
        def _(dve):
            steps = [0]

            def link(instruction):
                steps[0] += 1
                instruction.then_inc(dve_step, 1)
                dve.wait_ge(dve_step, steps[0])

            def gate_weights():
                dve.wait_ge(in_wg, 32)
                wi = wg_in[:, :, :].rearrange("p w (j n) -> p w j n", j=NPAIR)
                link(dve.tensor_tensor(wi[:, 1], wi[:, 1], wi[:, 2], ALU.add))
                link(dve.tensor_copy(wg_sb[:, :, :, 0, :], wi[:, 0:2]))
                link(dve.tensor_tensor(wg_r[:, :, :, :], wi[:, 0:2], wg_sb[:, :, :, 0, :], ALU.subtract))
                link(dve.tensor_copy(wg_sb[:, :, :, 1, :], wg_r[:, :, :, :]))
                dve.tensor_tensor(wg_sb[:, :, :, 2, :], wg_r[:, :, :, :], wg_sb[:, :, :, 1, :], ALU.subtract)\
                    .then_inc(wg_part, 1)

            def route_weights():
                dve.wait_ge(in_late, 64)
                link(dve.tensor_copy(gw3[:, :, 0, :], gw[:, :, :]))
                link(dve.tensor_tensor(gwr[:, :, :], gw[:, :, :], gw3[:, :, 0, :], ALU.subtract))
                link(dve.tensor_copy(gw3[:, :, 1, :], gwr[:, :, :]))
                dve.tensor_tensor(gw3[:, :, 2, :], gwr[:, :, :], gw3[:, :, 1, :], ALU.subtract).then_inc(gw_ok, 1)

            def weight_sizes(p, i):
                c0, c1 = piece(p, i)
                dve.wait_ge(in_up[p][i], 16)
                dve.tensor_reduce(wmax[:, p, i:i + 1], w_up[:, c0:c1].rearrange("p c w k f -> p (c w k f)"), AX.X,
                                  ALU.max, apply_absolute_value=True).then_inc(wmax_ok, 1)

            def weight_scales(p):
                dve.wait_ge(wall_ok, p + 1)
                link(dve.tensor_reduce(wpow[:, p, 1:2], wall[:, p, :], AX.X, ALU.max))
                link(dve.tensor_scalar(wpow[:, p, 1:2], wpow[:, p, 1:2], 1e-30, None, ALU.max))
                link(dve.tensor_scalar(wpow[:, p, 0:1].bitcast(I32), wpow[:, p, 1:2].bitcast(I32), 0x7F800000, None,
                                       ALU.bitwise_and))
                link(dve.reciprocal(wpow[:, p, 1:2], wpow[:, p, 0:1]))
                link(dve.tensor_scalar(unscale[:, p, 0:1], wpow[:, p, 0:1], 0.5 / UPSCALE, None, ALU.mult))
                link(dve.tensor_scalar(unscale[:, p, 1:2], unscale[:, p, 0:1], unscale[:, p, 0:1], 2 / (1, WSCALE)[p],
                                       ALU.mult, ALU.mult))
                dve.tensor_scalar(wmul[:, p:p + 1], wpow[:, p, 1:2], MSCALE, None, ALU.mult).then_inc(wmul_ok, 1)

            def low_weights(c):
                p = part(c)
                dve.wait_ge(whi_ok, c + 1)
                dve.scalar_tensor_tensor(out=up16[:, c, 1].rearrange("p w k f -> p (w k f)"),
                                         in0=w_up[:, c].rearrange("p w k f -> p (w k f)"), scalar=wmul[:, p:p + 1],
                                         in1=up16[:, c, 0].rearrange("p w k f -> p (w k f)"),
                                         op0=ALU.mult, op1=ALU.subtract).then_inc(wlo_ok, 1)

            def row_stats(g):
                for b in range(GB * g, GB * g + GB):
                    dve.wait_ge(in_rows[b], 32)
                    steps[0] += 1
                    dve.bn_stats(st6[:, b, :], x_sb[:, b, :]).then_inc(dve_step, 1)
                steps[0] += 1
                dve.tensor_reduce(kmax[:, g:g + 1], ctx_sb[:, GB * g:GB * g + GB, :].rearrange("p b e -> p (b e)"), AX.X,
                                  ALU.max, apply_absolute_value=True).then_inc(dve_step, 1)
                dve.wait_ge(dve_step, steps[0])
                for b in range(GB * g, GB * g + GB):
                    last = dve.bn_aggr(mv[:, b, :], st6[:, b, :])
                last.then_inc(stats_ok, 1)

            def row_scales(g):
                dve.wait_ge(rstd_ok, 2 * g + 2)
                n = slice(GB * g, GB * g + GB)
                link(dve.tensor_scalar(kall[:, g:g + 1], kall[:, g:g + 1], 1e-30, None, ALU.max))
                link(dve.tensor_scalar(kpow[:, g, 0:1].bitcast(I32), kall[:, g:g + 1].bitcast(I32), 0x7F800000, None,
                                       ALU.bitwise_and))
                link(dve.reciprocal(kpow[:, g, 1:2], kpow[:, g, 0:1]))
                dve.tensor_scalar(kpow[:, g, 2:3], kpow[:, g, 1:2], KSCALE, None, ALU.mult)
                link(dve.tensor_scalar(kpow[:, g, 3:4], kpow[:, g, 0:1], 1 / KSCALE, None, ALU.mult))
                dve.tensor_scalar(kpow[:, g, 4:5], kpow[:, g, 3:4], RSUM, None, ALU.mult)
                link(dve.tensor_scalar(kpow[:, g, 5:6], kpow[:, g, 3:4], kpow[:, g, 3:4], RSUM, ALU.mult, ALU.mult))
                dve.scalar_tensor_tensor(out=nb[:, n], in0=mv[:, n, 0], scalar=-1.0, in1=rstd[:, n],
                                         op0=ALU.mult, op1=ALU.mult).then_inc(scales_ok, 1)

            def low_keys(g):
                for b in range(GB * g, GB * g + GB):
                    dve.wait_ge(k_hi, b + 1)
                    c = ctx_sb[:, b, :].rearrange("p (h i) -> p h i", i=DH)
                    dve.scalar_tensor_tensor(out=k3[:, b % 4, :, 1, :], in0=c, scalar=kpow[:, g, 2:3],
                                             in1=k3[:, b % 4, :, 0, :], op0=ALU.mult, op1=ALU.subtract)\
                        .then_inc(k_low, 1)

            def gates(b):
                g, r = divmod(b, GB)
                dve.wait_ge(T_full, T_AT["gates", b])
                dve.tensor_reduce(gred[:, r], pT[:, 0:192].rearrange("p (a s i) -> p a i s", a=2, s=3),
                                  AX.X, ALU.add).then_inc(gsum_ok, 1)
                dve.wait_ge(gsum_ok, b + 1)
                link(dve.scalar_tensor_tensor(out=gt1[:, r, :], in0=gred[:, r, 1, :], scalar=kpow[:, g, 3:4],
                                              in1=bias_sb[:, :], op0=ALU.mult, op1=ALU.add))
                if g >= 2:
                    dve.wait_ge(T_full, T_AT["gT", g - 2])
                dve.scalar_tensor_tensor(out=g_tm[:, g % 2, :, r, :],
                                         in0=gred[:, r, 0, :].rearrange("p (a h) -> p a h", a=2),
                                         scalar=1.0 / QSCALE, in1=gt1[:, r, :].rearrange("p (a h) -> p a h", a=2),
                                         op0=ALU.mult, op1=ALU.add).then_inc(gates_ok, 1)

            def gate_rows(g):
                dve.wait_ge(T_full, T_AT["gT", g])
                dve.tensor_copy(gT[:, :, :], pT[0:GB * NH, 0:2 * S].rearrange("p (a s) -> p a s", a=2))\
                    .then_inc(gT_ok, 1)

            def gate_scans(g):
                dve.wait_ge(gln_ok, g + 1)
                dve.wait_ge(gT_ok, g + 1)
                link(dve.scalar_tensor_tensor(out=lf[:, 0, :], in0=gT[:, 1, :], scalar=0.0, in1=gabs[:, 2, :],
                                              op0=ALU.min, op1=ALU.subtract))
                link(dve.tensor_tensor_scan(lf[:, 1, :], ones[:, :], lf[:, 0, :], 0.0, ALU.mult, ALU.add))
                if g >= 1:
                    dve.wait_ge(M_full, M_AT["aT", g - 1])
                if g >= 2:
                    dve.wait_ge(g_row_in, 16 * (g - 1))
                link(dve.tensor_tensor(aM[:, 0, :], gT[:, 0, :], lf[:, 1, :], ALU.subtract))
                link(dve.tensor_tensor_scan(Gm[:, g % 2, :], aM[:, 0, :], aM[:, 0, :], -3e38, ALU.max, ALU.max))
                dve.tensor_tensor(aM[:, 1, :], lf[:, 1, :], Gm[:, g % 2, :], ALU.add).then_inc(aM_ok, 1)

            def scores(n):
                dve.wait_ge(D_ok, n + 1)
                z = Z[:, n % 3].rearrange("p (j e) s -> p j e s", e=2)
                for e in range(2):
                    dve.wait_ge(qk_ok, 2 * n + e + 1)
                    dve.scalar_tensor_tensor(out=z[:, :, e, :], in0=pQK[e][:, :].rearrange("p (j s) -> p j s", s=S),
                                             scalar=CSCALE, in1=z[:, :, e, :], op0=ALU.mult, op1=ALU.mult)\
                        .then_inc(C_ok, 1)

            def head_sums(n):
                dve.wait_ge(pv_ok, n + 1)
                r, h0 = (n // 2) % 2, (n % 2) * UH
                pv = pPV[:, :].rearrange("p (h w) -> p h w", w=64)
                dve.tensor_reduce(U[:, r, h0:h0 + UH, :], pv[:, :, 0:2 * DH].rearrange("p h (s i) -> p h i s", s=2),
                                  AX.X, ALU.add)
                dve.tensor_copy(rs[:, r, h0:h0 + UH], pv[:, :, 3 * DH]).then_inc(pv_used, 1)

            def head_means(b):
                g, r = divmod(b, GB)
                dve.wait_ge(eM_ok, g + 1)
                dve.wait_ge(pv_used, 2 * b + 2)
                n = nrm[:, r]
                link(dve.scalar_tensor_tensor(out=n[:, 0, :], in0=rs[:, r, :], scalar=-1.0, in1=rs[:, r, :],
                                              op0=ALU.mult, op1=ALU.max))
                link(dve.scalar_tensor_tensor(out=n[:, 1, :], in0=n[:, 0, :], scalar=kpow[:, g, 4:5],
                                              in1=eM[:, g % 2, r * NH:(r + 1) * NH], op0=ALU.mult, op1=ALU.max))
                link(dve.tensor_scalar(n[:, 2, :], n[:, 1, :], EPS, None, ALU.add))
                link(dve.reciprocal(n[:, 3, :], n[:, 2, :]))
                link(dve.tensor_scalar(n[:, 4, :], n[:, 3, :], kpow[:, g, 5:6], None, ALU.mult))
                link(dve.tensor_tensor(hh[:, :, :], U[:, r], bc(n[:, 4, :], DH), ALU.mult))
                link(dve.tensor_reduce(hst[:, r, 0, :], hh[:, :, :], AX.X, ALU.add))
                dve.scalar_tensor_tensor(out=hm[:, r], in0=bc(hst[:, r, 0, :], DH), scalar=-1.0 / DH,
                                         in1=hh[:, :, :], op0=ALU.mult, op1=ALU.add).then_inc(hm_ok, 1)

            def head_variances(b):
                r = b % 2
                dve.wait_ge(hsq_ok, b + 1)
                dve.tensor_reduce(hst[:, r, 1, :], hsq[:, r], AX.X, ALU.add).then_inc(hvar_ok, 1)

            def residual(b):
                dve.wait_ge(ho_ok, b + 1)
                link(dve.tensor_tensor(x1[:, b, :], x_sb[:, b, :], hsq[:, b % 2].rearrange("p h i -> p (h i)"), ALU.add))
                link(dve.bn_stats(st6[:, B + b, :], x1[:, b, :]))
                dve.bn_aggr(mv[:, B + b, :], st6[:, B + b, :]).then_inc(stats2_ok, 1)

            def row_offset(b):
                n = slice(B + b, B + b + 1)
                dve.wait_ge(rstd2_ok, b + 1)
                dve.scalar_tensor_tensor(out=nb[:, n], in0=mv[:, n, 0], scalar=-1.0, in1=rstd[:, n],
                                         op0=ALU.mult, op1=ALU.mult).then_inc(nb2_ok, 1)

            def route(g):
                r = g % 2
                dve.wait_ge(M_full, M_AT["logits", g])
                dve.tensor_reduce(lgs[:, r], pM[:, 0:128].rearrange("p (b w) -> p b w", b=GB)[:, :, 0:3 * (NEX + 1)]
                                  .rearrange("p b (s e) -> p b e s", s=3), AX.X, ALU.add).then_inc(lgs_ok, 1)
                dve.wait_ge(lgs_ok, g + 1)
                link(dve.tensor_scalar(lg[:, r], lgs[:, r], 1 / QSCALE, None, ALU.mult))
                l = lg[:, r, :, 0:NEX]
                dve.tensor_reduce(nmx[:, r, :], l, AX.X, ALU.max, negate=True).then_inc(nmx_ok, 1)
                gt, eq, beat = (cmpt[:, i].rearrange("p b (e j) -> p b e j", j=NEX) for i in range(3))
                for b in range(GB):
                    lj = l[:, b, :].unsqueeze(1).to_broadcast([P, NEX, NEX])
                    le = l[:, b, :].unsqueeze(2).to_broadcast([P, NEX, NEX])
                    dve.tensor_tensor(gt[:, b], lj, le, ALU.is_gt)
                    link(dve.tensor_tensor(eq[:, b], lj, le, ALU.is_equal))
                for b in range(GB):
                    last = dve.tensor_tensor(beat[:, b], eq[:, b], low[:, :, :], ALU.mult)
                link(last)
                link(dve.tensor_tensor(gt, gt, beat, ALU.add))
                dve.tensor_reduce(rank[:, r, 0], gt, AX.X, ALU.add)

            def route_part2(g):
                r = g % 2
                dve.wait_ge(ex_ok, 2 * GB * (g + 1))
                link(dve.tensor_scalar(esum[:, r, :, 1], ex[:, r, :, NEX], 1.0, None, ALU.add))
                link(dve.reciprocal(rcp[:, r], esum[:, r]))
                link(dve.scalar_tensor_tensor(out=rank[:, r, 1], in0=rank[:, r, 0], scalar=2.0,
                                              in1=ex[:, r, :, 0:NEX], op0=ALU.is_lt, op1=ALU.mult))
                for b in range(GB):
                    last = dve.tensor_scalar(rank[:, r, 0, b, :], rank[:, r, 1, b, :], rcp[:, r, b, 0:1], WSCALE,
                                             ALU.mult, ALU.mult)
                link(last)
                if g >= 2:
                    dve.wait_ge(M_full, M_AT["cT", g - 2])
                link(dve.tensor_copy(c16[:, r, :, 0, :], rank[:, r, 0]))
                dve.tensor_tensor(c16[:, r, :, 1, :], rank[:, r, 0], c16[:, r, :, 0, :], ALU.subtract)\
                    .then_inc(c16_ok, 1)

            def features(n):
                g, c = divmod(n, SLOTS)
                m = rows(c)
                up1, up2 = pU[n % 2][0:m, 0:TOK], pU[n % 2][0:m, TOK:2 * TOK]
                t, p, h = s_ff[0:m, n % 2, :], p_ff[0:m, n % 2, :], h_ff[0:m, n % 3, :]
                factor = unscale[0:m, part(c), 1:2]
                dve.wait_ge(s_ok, n + 1)
                if c < NC_SH:
                    link(dve.scalar_tensor_tensor(out=p, in0=t, scalar=1.0, in1=up1, op0=ALU.add, op1=ALU.mult))
                else:
                    f = c - NC_SH
                    dve.wait_ge(cw_ok, (NC_EX + 1) // 2 * g + f // 2 + 1)
                    link(dve.scalar_tensor_tensor(out=p, in0=t, scalar=1.0, in1=cw[:, f, :], op0=ALU.add, op1=ALU.mult))
                    link(dve.tensor_tensor(p, p, up1, ALU.mult))
                if n >= 3:
                    dve.wait_ge(dn_used, n - 2)
                dve.scalar_tensor_tensor(out=h, in0=p, scalar=factor, in1=up2, op0=ALU.mult, op1=ALU.mult)\
                    .then_inc(h_ok, 1)

            def shared_out(g):
                dve.wait_ge(dn_used, SLOTS * g + NC_SH)
                for b in range(GB):
                    n = GB * g + b
                    dve.scalar_tensor_tensor(out=y_sb[:, n, :], in0=pD[:, b * E:(b + 1) * E],
                                             scalar=rcp[:, g % 2, b, 1:2], in1=x1[:, n, :],
                                             op0=ALU.mult, op1=ALU.add).then_inc(y_ok, 1)

            def final_out(g):
                dve.wait_ge(dn_used, SLOTS * (g + 1))
                dve.wait_ge(y_ok, GB * (g + 1))
                for b in range(GB):
                    n = GB * g + b
                    dve.tensor_tensor(o_sb[:, n, :], y_sb[:, n, :], pD[:, b * E:(b + 1) * E], ALU.add).then_inc(o_ok, 1)

            dve.wait_ge(pool_const, 5)
            for t in range(END):
                if (g := group_at(t, STATS)) is not None:
                    row_stats(g)
                if t == STATS + 1:
                    gate_weights()
                    route_weights()
                if (g := group_at(t, FFN + NC_SH + 2)) is not None:
                    shared_out(g)
                if (g := group_at(t, FFN + SLOTS + 2)) is not None:
                    final_out(g)
                if (g := group_at(t, SCALES)) is not None:
                    row_scales(g)
                if (g := group_at(t, LOWS)) is not None:
                    low_keys(g)
                for b in range(GB):
                    if (g := group_at(t, GATES[b] + 1)) is not None:
                        gates(GB * g + b)
                if (g := group_at(t, GATE_ROWS + 1)) is not None:
                    gate_rows(g)
                if (g := group_at(t, SCANS)) is not None:
                    gate_scans(g)
                for u in range(UNITS):
                    if (g := group_at(t, SCORES + 5 + UNIT * u)) is not None:
                        head_sums(UNITS * g + u)
                    if (g := group_at(t, SCORES + 1 + UNIT * u)) is not None:
                        scores(UNITS * g + u)
                for b in range(GB):
                    if (g := group_at(t, NORM[b])) is not None:
                        head_means(GB * g + b)
                    if (g := group_at(t, NORM[b] + 2)) is not None:
                        head_variances(GB * g + b)
                    if (g := group_at(t, NORM[b] + 4)) is not None:
                        residual(GB * g + b)
                    if (g := group_at(t, NORM[b] + 6)) is not None:
                        row_offset(GB * g + b)
                if (g := group_at(t, LOGITS + 1)) is not None:
                    route(g)
                if (g := group_at(t, LOGITS + 3)) is not None:
                    route_part2(g)
                for p in range(2):
                    for i in range(PIECES):
                        if t == SIZES[p][i]:
                            weight_sizes(p, i)
                    if t == WSCALES[p]:
                        weight_scales(p)
                if SPLIT + 1 <= t < SPLIT + 1 + SLOTS:
                    low_weights(t - SPLIT - 1)
                if (n := chunk_at(t, 1)) is not None:
                    features(n)

        @block.tensor
        def _(pe):
            read = {"k": kT_ok, "q": qT_ok, "gates": gsum_ok, "gT": gT_ok, "aT": eM_ok, "x2": x2T_ok,
                    "logits": lgs_ok, "cT": cT_ok}
            units = [0]
            spreads = [0]

            def free(before, key):
                if before[key] is not None:
                    name, n = before[key]
                    pe.wait_ge(read[name], n + 1)

            def score_bank_free(e):
                if units[0]:
                    pe.wait_ge(C_ok, 2 * (units[0] - 1) + e + 1)
                if spreads[0]:
                    pe.wait_ge(cw_ok, spreads[0])

            def columns(source, o):
                for j in range(NPAIR):
                    last = pe.transpose(o[:, j * S:(j + 1) * S], source[:, 2 * j:2 * j + 2].rearrange("p h s i -> p (h s i)"),
                                        id16[:, :])
                return last

            def key_columns(b):
                free(T_BEFORE, ("k", b))
                pe.wait_ge(k_low, b + 1)
                columns(k3[:, b % 4], pT16).then_inc(T_full, 1)

            def query_columns(b):
                free(M_BEFORE, ("q", b))
                pe.wait_ge(q_low, b + 1)
                columns(q3[:, b % 2], pM16).then_inc(M_full, 1)

            def gates(b):
                free(T_BEFORE, ("gates", b))
                pe.wait_ge(qT_ok, b + 1)
                pe.wait_ge(kT_ok, b + 1)
                for w, operand in enumerate((qT, kT)):
                    for j in range(NPAIR):
                        last = pe.matmul(pT[:, 96 * w:96 * w + 96], operand[:, b % 4, j, :],
                                         wg_sb[:, w, j].rearrange("p s n -> p (s n)"),
                                         start=(j == 0), stop=(j == NPAIR - 1))
                last.then_inc(T_full, 1)

            def gate_rows(g):
                free(T_BEFORE, ("gT", g))
                pe.wait_ge(gates_ok, GB * (g + 1))
                for a in range(2):
                    last = pe.transpose(pT[0:GB * NH, a * S:(a + 1) * S],
                                        g_tm[:, g % 2, a].rearrange("p b h -> p (b h)"), id32[:, :])
                last.then_inc(T_full, 1)

            def gate_columns(g):
                free(M_BEFORE, ("aT", g))
                pe.wait_ge(aM_ok, g + 1)
                for a in range(2):
                    last = pe.transpose(pM[:, 64 * a:64 * a + GB * NH], aM[:, a, :], id32[0:GB * NH, 0:GB * NH])
                last.then_inc(M_full, 1)

            def scores(n):
                b, h0 = n // 2, (n % 2) * UH
                for e in range(2):
                    score_bank_free(e)
                    for i in range(UH // 2):
                        j, base = (h0 + 2 * i) // 2, 64 * e
                        last = pe.matmul(pQK[e][:, i * S:(i + 1) * S], kT[base:base + 3 * DH, b % 4, j, :],
                                         qT[base:base + 3 * DH, b % 4, j, :], start=True, stop=True)
                    last.then_inc(qk_ok, 1)
                units[0] += 1

            def outputs(n):
                b, h0 = n // 2, (n % 2) * UH
                pe.wait_ge(Clo_ok, n + 1)
                if n >= 1:
                    pe.wait_ge(pv_used, n)
                for i in range(UH):
                    o = pPV[:, 64 * i:64 * i + 3 * DH + 1]
                    v = k3[:, b % 4, h0 + i].rearrange("p s i -> p (s i)")[:, 0:3 * DH + 1]
                    pe.matmul(o, Chi[:, n % 2, i, :], v, start=True, stop=False)
                    last = pe.matmul(o, Clo[:, n % 2, i, :], v, start=False, stop=True)
                last.then_inc(pv_ok, 1)

            def x2_columns(b):
                o, full, _ = x2_bank(b)
                free((T_BEFORE, M_BEFORE)[b % GB], ("x2", b))
                pe.wait_ge(x2_low, b + 1)
                for i in range(4):
                    last = pe.transpose(o[:, i * S:(i + 1) * S],
                                        x2hl[:, b % 2, i // 2, (i % 2) * P:(i % 2 + 1) * P], id16[:, :])
                last.then_inc(full, 1)

            def logits(g):
                free(M_BEFORE, ("logits", g))
                pe.wait_ge(x2T_ok, GB * (g + 1))
                pe.wait_ge(gw_ok, 1)
                for b in range(GB):
                    for i in range(4):
                        last = pe.matmul(pM[:, 64 * b:64 * b + 3 * (NEX + 1)],
                                         x2T[:, g % 2, i // 2, i % 2, b * S:(b + 1) * S],
                                         gw3[:, i % 2].rearrange("p s e -> p (s e)"), start=(i == 0), stop=(i == 3))
                last.then_inc(M_full, 1)

            def route_columns(g):
                free(M_BEFORE, ("cT", g))
                pe.wait_ge(c16_ok, g + 1)
                for b in range(GB):
                    last = pe.transpose(pM16[0:2 * NEX, b * S:(b + 1) * S],
                                        c16[:, g % 2, b].rearrange("p s e -> p (s e)"), id16[:, :])
                last.then_inc(M_full, 1)

            def spread(g, i):
                pe.wait_ge(cT_ok, g + 1)
                for e in range(2):
                    score_bank_free(e)
                    for f in range(4 * i + 2 * e, min(4 * i + 2 * e + 2, NC_EX)):
                        last = pe.matmul(pQK[e][:, (f % 2) * TOK:(f % 2 + 1) * TOK], sel[:, f * P:(f + 1) * P],
                                         cT[:, g % 2, :], start=True, stop=True)
                    last.then_inc(spread_ok, 1)
                spreads[0] += 2

            def expert_up(n):
                g, c = divmod(n, SLOTS)
                m = rows(c)
                if c == 0:
                    pe.wait_ge(x2T_ok, GB * (g + 1))
                if g == 0:
                    pe.wait_ge(wlo_ok, c + 1)
                if n >= 2:
                    pe.wait_ge(h_ok, n - 1)
                for w in range(2):
                    for kk in range(2):
                        for i, (a, part_x) in enumerate(((0, 0), (0, 1), (1, 0))):
                            last = pe.matmul(pU[n % 2][0:m, w * TOK:(w + 1) * TOK], up16[:, c, a, w, kk, 0:m],
                                             x2T[:, g % 2, part_x, kk, :], start=(kk == 0 and i == 0),
                                             stop=(kk == 1 and i == 2))
                last.then_inc(up_ok, 1)

            def expert_down(n):
                g, c = divmod(n, SLOTS)
                m = rows(c)
                if g == 0 and c in (0, NC_SH):
                    pe.wait_ge(in_dn[part(c)], 16)
                if c == 0 and g > 0:
                    pe.wait_ge(o_ok, GB * g)
                if c == NC_SH:
                    pe.wait_ge(y_ok, GB * (g + 1))
                pe.wait_ge(h_ok, n + 1)
                for b in range(GB):
                    last = pe.matmul(pD[:, b * E:(b + 1) * E], h_ff[0:m, n % 3, b * S:(b + 1) * S],
                                     w_dn[0:m, c, :], start=(b == 0 and c in (0, NC_SH)),
                                     stop=c in (NC_SH - 1, SLOTS - 1), skip_group_check=True)
                last.then_inc(dn_used, 1)

            pe.wait_ge(in_const, 32)
            pe.wait_ge(pool_const, 5)
            pe.wait_ge(wg_part, 1)
            pe.wait_ge(in_late, 64)
            for t in range(END):
                for b in range(GB):
                    if (g := group_at(t, K_COLS[b])) is not None:
                        key_columns(GB * g + b)
                    if (g := group_at(t, Q_COLS[b])) is not None:
                        query_columns(GB * g + b)
                    if (g := group_at(t, GATES[b])) is not None:
                        gates(GB * g + b)
                if (g := group_at(t, GATE_ROWS)) is not None:
                    gate_rows(g)
                if (g := group_at(t, GATE_COLS)) is not None:
                    gate_columns(g)
                for u in range(UNITS):
                    if (g := group_at(t, SCORES + UNIT * u)) is not None:
                        scores(UNITS * g + u)
                    if (g := group_at(t, SCORES + 4 + UNIT * u)) is not None:
                        outputs(UNITS * g + u)
                for b in range(GB):
                    if (g := group_at(t, X2_COLS[b])) is not None:
                        x2_columns(GB * g + b)
                if (g := group_at(t, LOGITS)) is not None:
                    logits(g)
                if (g := group_at(t, ROUTE_COLS)) is not None:
                    route_columns(g)
                for i in range(len(SPREAD)):
                    if (g := group_at(t, SPREAD[i])) is not None:
                        spread(g, i)
                if (n := chunk_at(t, 0)) is not None:
                    expert_up(n)
                if (n := chunk_at(t, 2)) is not None:
                    expert_down(n)


def constants():
    ident = np.eye(P, dtype=np.float32)
    expert = np.arange(NC_EX * P) // FM
    select = (np.arange(2 * NEX)[:, None] % NEX == expert[None, :]).astype(np.float16)
    lower = np.broadcast_to(np.tril(np.ones((NEX, NEX), np.float32), -1), (P, NEX, NEX))
    return {"ident": ident, "ident16": ident.astype(np.float16), "select": select,
            "lower": np.ascontiguousarray(lower)}


def layouts(a):
    out = {"x": a["x"], "ctx_in": a["ctx_2048"]}
    gates = np.concatenate([a["L0_xattn_Wi"], a["L0_xattn_Wf"]], axis=1)
    gates = gates.reshape(3, NPAIR, 2, DH, 2 * NH).transpose(0, 2, 3, 1, 4)
    wg = np.zeros((2, 4, DH, 3, NPAIR, 2 * NH), np.float32)
    for slot in (0, 2):
        wg[:, slot, :, 0] = gates[0]
    for w in (1, 2):
        for slot in (0, 1):
            wg[:, slot, :, w] = gates[w]
    out["wg"] = wg.reshape(P, 3, NPAIR * 2 * NH)
    out["bias_g"] = np.concatenate([a["L0_xattn_bi"], a["L0_xattn_bf"]])
    out["ln_scale"] = a["L0_xattn_ln_scale"]
    route = np.concatenate([a["L0_ffn_gate_w"], a["L0_ffn_shared_gate_w"]], axis=0)
    out["gate_w"] = route.T.reshape(2, P, NEX + 1).transpose(1, 0, 2)
    up = np.zeros((2, SLOTS * P, E), np.float32)
    for w in range(2):
        up[w, 0:FS] = a[f"L0_ffn_shared_fc{w + 1}"]
        up[w, NC_SH * P:] = a[f"L0_ffn_expert_fc{w + 1}"].reshape(NEX * FM, E)
    out["up"] = up.reshape(2, SLOTS, P, 2, P).transpose(1, 4, 0, 3, 2)
    down = np.zeros((SLOTS * P, E), np.float32)
    down[0:FS] = a["L0_ffn_shared_proj"].T
    down[NC_SH * P:] = a["L0_ffn_expert_proj"].transpose(0, 2, 1).reshape(NEX * FM, E)
    out["down"] = down.reshape(SLOTS, P, E).transpose(1, 0, 2)
    return {k: np.ascontiguousarray(v) for k, v in out.items()}


def kernel(**inputs):
    import concourse.bacc as bacc
    from concourse.bass_utils import run_bass_kernel_spmd

    arrays = layouts({k: np.asarray(v) for k, v in inputs.items()}) | constants()
    nc = bacc.Bacc("TRN2", target_bir_lowering=False, num_devices=1)
    args = {k: nc.dram_tensor(k, v.shape, mybir.dt.from_np(v.dtype), kind="ExternalInput").ap()
            for k, v in arrays.items()}
    out = nc.dram_tensor("out", (B, S, E), F32, kind="ExternalOutput").ap()
    build(nc, **args, out=out)
    r = run_bass_kernel_spmd(nc, [arrays], core_ids=[0])
    return r.results[0]["out"]
```

```python
from contextlib import ExitStack

import concourse.bass as bass
from concourse import mybir
import numpy as np

F32, F16, BF16, I32 = mybir.dt.float32, mybir.dt.float16, mybir.dt.bfloat16, mybir.dt.int32
ALU, ACT, AX = mybir.AluOpType, mybir.ActivationFunctionType, mybir.AxisListType
MAX = bass.bass_isa.ReduceOp.max

P = 128
B, S, E = 8, 128, 256
NH = 16
DH = E // NH
NEX, FM, FS = 8, 176, 704
FIRST = [0, 2, 4, 6, 8]
NG = len(FIRST) - 1
GB = 2
TOK = GB * S
NPAIR = NH // 2
NC_SH = -(-FS // P)
NC_EX = NEX * FM // P
SLOTS = NC_SH + NC_EX
REST = FS - (NC_SH - 1) * P
PAIRED = NC_SH - 1
assert 2 * REST == P
UH = 8
UNITS = NH // UH
UW = UH * S
LN_EPS, EPS = 1e-5, 1e-6
FAR = 1e30
QSCALE = 2.0 ** 11
KSCALE = 2.0 ** 13
CSCALE = 2.0 ** -16
RSUM = 1 / (QSCALE * CSCALE * DH ** 0.5)
MSCALE = 2.0 ** 14
UPSCALE = QSCALE * MSCALE
WSCALE = 2.0 ** 15
PIECES = 4

TICKS = 2
PERIOD = TICKS * SLOTS
PE_AT = dict(keys=[5, 7], queries=[6, 8], gates=[9, 10], gate_rows=12, gate_cols=17, scores=[15, 21, 24, 29],
             outputs=[25, 27, 34, 37], x2_cols=[44, 52], logits=53, route_cols=61, spread=[62, 69, 72], up=54,
             down=59)
ACT_AT = dict(key_parts=2, query_parts=5, keys=[6, 8], queries=[7, 9], forget=14, gate_cols=18, decays=[20, 20,
              21, 22, 26, 26, 30, 32], high=[23, 24, 29, 35], squares=[33, 42], x2=[42, 51], x2_cols=[44, 53],
              route=59, route_cols=62, spread=[63, 70, 72], tanh=56)
DVE_AT = dict(stats=0, scales=1, key_parts=5, gates=[10, 11], gate_rows=13, scans=15, scores=[22, 23, 28, 34],
              sums=[26, 28, 35, 37], means=[31, 42], variances=[35, 42], residual=[40, 48], offset=[42, 49],
              route=56, route2=60, features=56, shared=70, final=92, norms=[30, 39], ranks=57)
POOL_AT = dict(deviations=2, query_parts=5, maxima=[21, 22, 22, 28], low=[23, 24, 35, 36], heads=[37, 43],
               deviations2=[40, 44], x2=[43, 47], row=11)
ONCE = dict(gate_weights=3, route_weights=24)
SIZES = [[12, 13, 14, 15], [15, 16, 19, 20]]
ALL_MAX = [14, 23]
WSCALES = [16, 27]
SPLIT = [18, 21, 24, 24, 34, 34, 35, 38, 39, 46, 46, 48, 49, 50, 51, 51, 55]
START = [0, 34, 68, 102]
LATE = [PERIOD * g for g in range(NG)]
END = START[-1] + DVE_AT["final"] + 2


def gate_rows_of(c):
    return slice(0, REST if c == PAIRED else P)


def rows_in(c):
    return slice(REST if c == PAIRED else 0, P)


def size(g):
    return FIRST[g + 1] - FIRST[g]


def rows_of(g):
    return range(FIRST[g], FIRST[g + 1])


def group_of(b):
    g = next(g for g in range(NG) if b < FIRST[g + 1])
    return g, b - FIRST[g]


def group_at(t, offset, least=1):
    return next((g for g in range(NG) if START[g] + offset == t and size(g) >= least), None)


def late_at(t, offset, least=1):
    return next((g for g in range(NG) if LATE[g] + offset == t and size(g) >= least), None)


def chunk_at(t, offset):
    n, late = divmod(t - offset, TICKS)
    return n if late == 0 and 0 <= n < NG * SLOTS else None


def fills(bank):
    order = []
    for place, (step, at, i, of) in enumerate(bank):
        base = LATE if step in ("x2_cols", "logits", "route_cols", "spread") else START
        order += [(base[g] + at, place, (step, FIRST[g] + i if of == GB else of * g + i))
                  for g in range(NG) if of != GB or i < size(g)]
    keys = [key for _, _, key in sorted(order)]
    return dict(zip(keys, [None] + keys)), {key: i + 1 for i, key in enumerate(keys)}


def in_bank(step, i, of):
    at = PE_AT[step]
    return step, at if isinstance(at, int) else at[i * len(at) // of], i, of


SPREADS = -(-NC_EX // 2)
T_BEFORE, T_AT = fills([in_bank("gates", 0, GB), in_bank("keys", 0, GB), in_bank("keys", 1, GB),
                        in_bank("gate_rows", 0, 1), in_bank("x2_cols", 0, GB)]
                       + [in_bank("spread", j, SPREADS) for j in range(0, SPREADS, 2)])
M_BEFORE, M_AT = fills([in_bank("queries", 0, GB), in_bank("queries", 1, GB), in_bank("gates", 1, GB),
                        in_bank("gate_cols", 0, 1), in_bank("x2_cols", 1, GB), in_bank("logits", 0, 1),
                        in_bank("route_cols", 0, 1)]
                       + [in_bank("spread", j, SPREADS) for j in range(1, SPREADS, 2)])


def build(nc, x, ctx_in, wg, bias_g, ln_scale, gate_w, up, down, ident, ident16, select, lower, out):
    with ExitStack() as stack:
        def sb(name, shape, dt=F32):
            return stack.enter_context(nc.sbuf_tensor(name, shape, dt))

        def sem(name):
            return stack.enter_context(nc.semaphore(name))

        def bank(name):
            return stack.enter_context(nc.psum_tensor(name, [P, 512], F32))

        x_sb = sb("x_sb", [P, B, E])
        ctx_sb = sb("ctx_sb", [P, B, E])
        id32 = sb("id32", [P, P])
        id16 = sb("id16", [P, P], F16)
        sel = sb("sel", [2 * NEX, NC_EX * P], F16)
        low = sb("low", [P, NEX, NEX])
        bias_sb = sb("bias_sb", [P, 2 * NH])
        lnsc = sb("lnsc", [P, E])
        gw = sb("gw", [P, 2, NEX + 1])
        gwr = sb("gwr", [P, 2, NEX + 1])
        gw3 = sb("gw3", [P, 2, 3, NEX + 1], BF16)
        wg_in = sb("wg_in", [P, 3, NPAIR * 2 * NH])
        wg_sb = sb("wg_sb", [P, 2, NPAIR, 3, 2 * NH], BF16)
        wg_r = sb("wg_r", [P, 2, NPAIR, 2 * NH])
        w_up = sb("w_up", [P, SLOTS, 2, 2, P])
        up16 = sb("up16", [P, SLOTS, 2, 2, 2, P], F16)
        w_dn = sb("w_dn", [P, SLOTS, E])
        wmax = sb("wmax", [P, 2, PIECES])
        wall = sb("wall", [P, 2, PIECES])
        wpow = sb("wpow", [P, 2, 2])
        wmul = sb("wmul", [P, 2])
        unscale = sb("unscale", [P, 2, 3])
        half = sb("half", [P, NH])
        ones = sb("ones", [GB * NH, S])

        st6 = sb("st6", [P, 2 * B, 6])
        mv = sb("mv", [P, 2 * B, 2])
        ve = sb("ve", [P, 2 * B])
        rstd = sb("rstd", [P, 2 * B])
        nb = sb("nb", [P, 2 * B])
        kmax = sb("kmax", [P, NG])
        kall = sb("kall", [P, NG])
        kpow = sb("kpow", [P, NG, 6])
        qs = sb("qs", [P, 2, E])
        q3 = sb("q3", [P, 2, NH, 4, DH], F16)
        k3 = sb("k3", [P, 4, NH, 4, DH], F16)
        qT = sb("qT", [P, 4, NPAIR, S], F16)
        kT = sb("kT", [P, 4, NPAIR, S], F16)
        gred = sb("gred", [P, 2, 2, 2 * NH])
        gt1 = sb("gt1", [P, 2, 2 * NH])
        g_tm = sb("g_tm", [P, 2, 2, GB, NH])
        gT = sb("gT", [GB * NH, 2, S])
        gabs = sb("gabs", [GB * NH, 3, S])
        lf = sb("lf", [GB * NH, 2, S])
        aM = sb("aM", [GB * NH, 2, S])
        Gm = sb("Gm", [GB * NH, 2, S])
        Grow = sb("Grow", [1, GB * NH * S])
        a_tm = sb("a_tm", [P, 2, GB * NH])
        eM = sb("eM", [P, 2, GB * NH])
        Z = sb("Z", [P, 3, UH, S])
        Chi = sb("Chi", [P, 2, UH, S], F16)
        Clo = sb("Clo", [P, 2, UH, S], F16)
        U = sb("U", [P, 2, NH, DH])
        rs = sb("rs", [P, 2, NH])
        nrm = sb("nrm", [P, 2, 5, NH])
        hh = sb("hh", [P, NH, DH])
        hm = sb("hm", [P, 2, NH, DH])
        hsq = sb("hsq", [P, 2, NH, DH])
        hst = sb("hst", [P, 2, 4, NH])
        x1 = x_sb
        x2hl = sb("x2hl", [P, 2, 2, E], F16)

        lgs = sb("lgs", [P, 2, GB, NEX + 1])
        lg = sb("lg", [P, 2, GB, NEX + 1])
        nmx = sb("nmx", [P, 2, GB])
        ex = sb("ex", [P, 2, GB, NEX + 1])
        esum = sb("esum", [P, 2, GB, 2])
        rcp = sb("rcp", [P, 2, GB, 2])
        cmpt = sb("cmpt", [P, 3, GB, NEX * NEX])
        rank = sb("rank", [P, 2, 2, GB, NEX])
        c16 = sb("c16", [P, 2, GB, 2, NEX], F16)
        early = w_up[:, 0:NC_SH].rearrange("p c w k f -> p (c w k f)")
        x2 = early[:, 0:2 * E].rearrange("p (r e) -> p r e", r=2)
        h_ff = early[:, 512:1280].rearrange("p (r t) -> p r t", r=3)
        x2T = early[:, 1280:2304].bitcast(F16).rearrange("p (r a k t) -> p r a k t", r=2, a=2, k=2)
        cT = early[0:2 * NEX, 2304:2560].bitcast(F16).rearrange("p (r t) -> p r t", r=2)
        late = w_up[:, NC_SH:].rearrange("p c w k f -> p (c w k f)")
        cw = late[:, 0:NC_EX * TOK].rearrange("p (f t) -> p f t", f=NC_EX)
        s_ff = wg_in[:, 0:2, :]
        p_ff = wg_r[:, :, :, :].rearrange("p w j n -> p w (j n)")
        y_sb, o_sb = x_sb, ctx_sb

        pT = bank("pT")
        pM = bank("pM")
        pT16, pM16 = pT[:, :].bitcast(F16), pM[:, :].bitcast(F16)
        pQK = [bank("pQK0"), bank("pQK1")]
        pPV = bank("pPV")
        pU = [bank("pU0"), bank("pU1")]
        pD = bank("pD")

        in_rows = [sem(f"in_rows{b}") for b in range(B)]
        in_const, in_wg, in_late = sem("in_const"), sem("in_wg"), sem("in_late")
        in_up = [[sem(f"in_up{p}_{i}") for i in range(PIECES)] for p in range(2)]
        in_dn = [sem(f"in_dn{p}") for p in range(2)]
        g_row_in, stored = sem("g_row_in"), sem("stored")
        dve_step, act_step, pool_step = sem("dve_step"), sem("act_step"), sem("pool_step")
        pool_const, wg_part, gw_ok = sem("pool_const"), sem("wg_part"), sem("gw_ok")
        wmax_ok, wall_ok, wmul_ok = sem("wmax_ok"), sem("wall_ok"), sem("wmul_ok")
        whi_ok, wlo_ok = sem("whi_ok"), sem("wlo_ok")
        stats_ok = sem("stats_ok")
        rstd_ok = sem("rstd_ok")
        scales_ok = sem("scales_ok")
        q_hi, k_hi, q_low, k_low = sem("q_hi"), sem("k_hi"), sem("q_low"), sem("k_low")
        T_full, M_full = sem("T_full"), sem("M_full")
        qT_ok, kT_ok = sem("qT_ok"), sem("kT_ok")
        gsum_ok, gates_ok, gT_ok, gln_ok, aM_ok = sem("gsum_ok"), sem("gates_ok"), sem("gT_ok"), sem("gln_ok"), sem("aM_ok")
        a_ok, eM_ok, z_ok, D_ok = sem("a_ok"), sem("eM_ok"), sem("z_ok"), sem("D_ok")
        qk_ok, C_ok, Chi_ok, Clo_ok, pv_ok, pv_used = (sem("qk_ok"), sem("C_ok"), sem("Chi_ok"), sem("Clo_ok"),
                                                       sem("pv_ok"), sem("pv_used"))
        hm_ok, hsq_ok, hvar_ok, ho_ok = sem("hm_ok"), sem("hsq_ok"), sem("hvar_ok"), sem("ho_ok")
        stats2_ok, rstd2_ok, nb2_ok = sem("stats2_ok"), sem("rstd2_ok"), sem("nb2_ok")
        x2_hi, x2_low, x2T_ok = sem("x2_hi"), sem("x2_low"), sem("x2T_ok")
        lgs_ok, nmx_ok, ex_ok, c16_ok, cT_ok = sem("lgs_ok"), sem("nmx_ok"), sem("ex_ok"), sem("c16_ok"), sem("cT_ok")
        cw_ok = sem("cw_ok")
        up_ok = sem("up_ok")
        s_ok, h_ok = sem("s_ok"), sem("h_ok")
        dn_used = sem("dn_used")
        y_ok, o_ok = sem("y_ok"), sem("o_ok")

        block = stack.enter_context(nc.Block())

        def bc(ap, n):
            return ap.unsqueeze(2).to_broadcast([ap.shape[0], ap.shape[1], n])

        def x2_bank(b):
            return (pT16, T_full, T_AT["x2_cols", b]) if group_of(b)[1] == 0 else (pM16, M_full, M_AT["x2_cols", b])

        def gates_bank(b):
            return (pT, T_full, T_AT["gates", b]) if group_of(b)[1] == 0 else (pM, M_full, M_AT["gates", b])

        def spread_bank(g, j):
            n = SPREADS * g + j
            return (pT, T_full, T_AT["spread", n]) if j % 2 == 0 else (pM, M_full, M_AT["spread", n])

        PART = [(0, NC_SH), (NC_SH, SLOTS)]

        def part(c):
            return int(c >= NC_SH)

        def piece(p, i):
            lo, hi = PART[p]
            return lo + (hi - lo) * i // PIECES, lo + (hi - lo) * (i + 1) // PIECES

        @block.sync
        def _(sp):
            for b in rows_of(0):
                sp.dma_start(x_sb[:, b, :], x[b]).then_inc(in_rows[b], 16)
            sp.dma_start(id16[:, :], ident16).then_inc(in_const, 16)
            sp.dma_start(id32[:, :], ident).then_inc(in_const, 16)
            for p, (lo, hi) in enumerate(PART):
                for i in range(PIECES):
                    c0, c1 = piece(p, i)
                    if (p, i) == (1, 3):
                        sp.wait_ge(g_row_in, 16)
                    sp.dma_start(w_up[:, c0:c1], up[c0:c1].rearrange("c p w k f -> p c w k f")).then_inc(in_up[p][i], 16)
                if p == 0:
                    sp.dma_start(lnsc[:, :], ln_scale.partition_broadcast(P)).then_inc(in_late, 16)
                    sp.dma_start(gw[:, :, :], gate_w).then_inc(in_late, 16)
                    sp.dma_start(sel[:, :], select).then_inc(in_late, 16)
                    sp.dma_start(low[:, :, :], lower).then_inc(in_late, 16)
                for b in (rows_of(1), range(FIRST[2], B))[p]:
                    sp.dma_start(x_sb[:, b, :], x[b]).then_inc(in_rows[b], 16)
                    sp.dma_start(ctx_sb[:, b, :], ctx_in[b]).then_inc(in_rows[b], 16)
                sp.dma_start(w_dn[:, lo:hi, :], down[:, lo:hi, :]).then_inc(in_dn[p], 16)
            for b in range(B):
                sp.wait_ge(o_ok, b + 1)
                sp.dma_start(out[b], o_sb[:, b, :]).then_inc(stored, 16)
            sp.wait_ge(stored, 16 * B)

        @block.gpsimd
        def _(pool):
            steps = [0]

            def link(instruction):
                steps[0] += 1
                instruction.then_inc(pool_step, 1)
                pool.wait_ge(pool_step, steps[0])

            def row_deviations(g):
                n = slice(FIRST[g], FIRST[g + 1])
                pool.wait_ge(stats_ok, g + 1)
                link(pool.tensor_scalar(ve[:, n], mv[:, n, 1], LN_EPS, QSCALE ** -2, ALU.add, ALU.mult))
                pool.tensor_tensor(rstd[:, n], ve[:, n], half[:, 0:size(g)], ALU.pow).then_inc(rstd_ok, 1)
                pool.partition_all_reduce(kall[:, g:g + 1], kmax[:, g:g + 1], P, MAX).then_inc(rstd_ok, 1)

            def low_queries(g):
                for b in rows_of(g):
                    pool.wait_ge(q_hi, b + 1)
                    q = qs[:, b % 2, :].rearrange("p (h i) -> p h i", i=DH)
                    pool.tensor_tensor(q3[:, b % 2, :, 2, :], q, q3[:, b % 2, :, 0, :], ALU.subtract).then_inc(q_low, 1)

            def maxima_row(g):
                pool.wait_ge(aM_ok, g + 1)
                if g >= 1:
                    pool.wait_ge(z_ok, UNITS * FIRST[g])
                pool.dma_start(Grow[0:1, 0:size(g) * NH * S], Gm[0:size(g) * NH, g % 2, :]).then_inc(g_row_in, 16)

            def maxima(n):
                g, _ = group_of(n // UNITS)
                u = n - UNITS * FIRST[g]
                if u == 0:
                    pool.wait_ge(g_row_in, 16 * (g + 1))
                if n >= 3:
                    pool.wait_ge(Clo_ok, n - 2)
                z = Z[:, n % 3]
                link(pool.partition_broadcast(z.rearrange("p h s -> p (h s)"), Grow[0:1, u * UW:(u + 1) * UW], P))
                pool.affine_select(out=z, in_=z, compare_op=ALU.is_ge, fill=FAR, base=0,
                                   pattern=[[0, UH], [1, S]], channel_multiplier=-1).then_inc(z_ok, 1)

            def low_scores(n):
                pool.wait_ge(Chi_ok, n + 1)
                if n >= 2:
                    pool.wait_ge(pv_ok, n - 1)
                pool.tensor_tensor(Clo[:, n % 2], Z[:, n % 3], Chi[:, n % 2], ALU.subtract).then_inc(Clo_ok, 1)

            def scaled_heads(b):
                r = b % 2
                pool.wait_ge(hvar_ok, b + 1)
                if b == 0:
                    pool.wait_ge(in_late, 64)
                link(pool.tensor_scalar(hst[:, r, 2, :], hst[:, r, 1, :], 1.0 / DH, EPS, ALU.mult, ALU.add))
                link(pool.tensor_tensor(hst[:, r, 3, :], hst[:, r, 2, :], half[:, :], ALU.pow))
                link(pool.tensor_tensor(hsq[:, r], hm[:, r], bc(hst[:, r, 3, :], DH), ALU.mult))
                h = hsq[:, r].rearrange("p h i -> p (h i)")
                pool.tensor_tensor(h, h, lnsc[:, :], ALU.mult).then_inc(ho_ok, 1)

            def row_deviation2(b):
                n = slice(B + b, B + b + 1)
                pool.wait_ge(stats2_ok, b + 1)
                link(pool.tensor_scalar(ve[:, n], mv[:, n, 1], LN_EPS, QSCALE ** -2, ALU.add, ALU.mult))
                pool.tensor_tensor(rstd[:, n], ve[:, n], half[:, 0:1], ALU.pow).then_inc(rstd2_ok, 1)

            def low_rows(b):
                pool.wait_ge(x2_hi, b + 1)
                pool.tensor_tensor(x2hl[:, b % 2, 1, :], x2[:, b % 2, :], x2hl[:, b % 2, 0, :], ALU.subtract)\
                    .then_inc(x2_low, 1)

            def weight_max(p):
                pool.wait_ge(wmax_ok, PIECES * (p + 1))
                pool.partition_all_reduce(wall[:, p, :], wmax[:, p, :], P, MAX).then_inc(wall_ok, 1)

            pool.memset(half[:, :], -0.5).then_inc(pool_const, 1)
            pool.memset(ones[:, :], 1.0).then_inc(pool_const, 1)
            pool.memset(q3[:, :, :, 3, :], 0.0).then_inc(pool_const, 1)
            pool.memset(k3[:, :, :, 3, 1:DH], 0.0).then_inc(pool_const, 1)
            pool.memset(k3[:, :, :, 3, 0:1], 1.0).then_inc(pool_const, 1)
            pool.wait_ge(pool_const, 5)
            for t in range(END):
                if (g := group_at(t, POOL_AT["deviations"])) is not None:
                    row_deviations(g)
                if (g := group_at(t, POOL_AT["query_parts"])) is not None:
                    low_queries(g)
                for u in range(GB * UNITS):
                    if (g := group_at(t, POOL_AT["low"][u], u // UNITS + 1)) is not None:
                        low_scores(UNITS * FIRST[g] + u)
                for b in range(GB):
                    if (g := late_at(t, POOL_AT["heads"][b], b + 1)) is not None:
                        scaled_heads(FIRST[g] + b)
                    if (g := late_at(t, POOL_AT["deviations2"][b], b + 1)) is not None:
                        row_deviation2(FIRST[g] + b)
                    if (g := late_at(t, POOL_AT["x2"][b], b + 1)) is not None:
                        low_rows(FIRST[g] + b)
                for u in range(GB * UNITS):
                    if u == 0 and (g := group_at(t, POOL_AT["row"])) is not None:
                        maxima_row(g)
                    if (g := group_at(t, POOL_AT["maxima"][u], u // UNITS + 1)) is not None:
                        maxima(UNITS * FIRST[g] + u)
                for p in range(2):
                    if t == ALL_MAX[p]:
                        weight_max(p)

        @block.scalar
        def _(act):
            steps = [0]

            def link(instruction):
                steps[0] += 1
                instruction.then_inc(act_step, 1)
                act.wait_ge(act_step, steps[0])

            for b in rows_of(0):
                act.dma_start(ctx_sb[:, b, :], ctx_in[b]).then_inc(in_rows[b], 16)
            act.dma_start(wg_in[:, :, :], wg).then_inc(in_wg, 16)
            act.dma_start(bias_sb[:, :], bias_g.partition_broadcast(P)).then_inc(in_wg, 16)
            act.wait_ge(pool_const, 5)
            link(act.activation(nrm[:, 0, 4, :], half[:, :], ACT.Exp))

            def high_keys(g):
                act.wait_ge(scales_ok, g + 1)
                for b in rows_of(g):
                    if b >= 2:
                        act.wait_ge(q_low, b - 1)
                    act.activation(qs[:, b % 2, :], x_sb[:, b, :], ACT.Identity, bias=nb[:, b:b + 1],
                                   scale=rstd[:, b:b + 1]).then_inc(act_step, 1)
                    steps[0] += 1
                for b in rows_of(g):
                    if b >= 4:
                        act.wait_ge(pv_ok, 2 * (b - 3))
                    c = ctx_sb[:, b, :].rearrange("p (h i) -> p h i", i=DH)
                    act.activation(k3[:, b % 4, :, 0:4:2, :], c.unsqueeze(2).to_broadcast([P, NH, 2, DH]), ACT.Copy,
                                   scale=kpow[:, g, 2:3]).then_inc(k_hi, 1)

            def high_queries(g):
                act.wait_ge(act_step, steps[0])
                for b in rows_of(g):
                    if b >= 2:
                        act.wait_ge(M_full, M_AT["queries", b - 2])
                    q = qs[:, b % 2, :].rearrange("p (h i) -> p h i", i=DH)
                    act.activation(q3[:, b % 2, :, 0:2, :], q.unsqueeze(2).to_broadcast([P, NH, 2, DH]), ACT.Copy)\
                        .then_inc(q_hi, 1)

            def key_columns(b):
                act.wait_ge(T_full, T_AT["keys", b])
                if b >= 4:
                    act.wait_ge(qk_ok, (b - 3) * 4)
                act.activation(kT[:, b % 4].rearrange("p j s -> p (j s)"), pT16, ACT.Copy).then_inc(kT_ok, 1)

            def query_columns(b):
                act.wait_ge(M_full, M_AT["queries", b])
                if b >= 4:
                    act.wait_ge(qk_ok, (b - 3) * 4)
                act.activation(qT[:, b % 4].rearrange("p j s -> p (j s)"), pM16, ACT.Copy).then_inc(qT_ok, 1)

            def forget_logs(g):
                act.wait_ge(gT_ok, g + 1)
                m = size(g) * NH
                link(act.activation(gabs[0:m, 0, :], gT[0:m, 1, :], ACT.Abs))
                link(act.activation(gabs[0:m, 1, :], gabs[0:m, 0, :], ACT.Exp, scale=-1.0))
                act.activation(gabs[0:m, 2, :], gabs[0:m, 1, :], ACT.Ln, bias=1.0).then_inc(gln_ok, 1)

            def gate_columns(g):
                act.wait_ge(M_full, M_AT["gate_cols", g])
                if g >= 2:
                    act.wait_ge(hm_ok, FIRST[g - 1])
                m = size(g) * NH
                act.activation(a_tm[:, g % 2, 0:m], pM[:, 0:m], ACT.Copy).then_inc(a_ok, 1)
                act.activation(eM[:, g % 2, 0:m], pM[:, 64:64 + m], ACT.Exp, scale=-1.0).then_inc(eM_ok, 1)

            def decays(n, k):
                g, _ = group_of(n // UNITS)
                u = n - UNITS * FIRST[g]
                if k == 0:
                    act.wait_ge(z_ok, n + 1)
                    act.wait_ge(a_ok, g + 1)
                for i in range(k * UH // 2, (k + 1) * UH // 2):
                    h = u * UH + i
                    last = act.activation(Z[:, n % 3, i, :], Z[:, n % 3, i, :], ACT.Exp,
                                          bias=a_tm[:, g % 2, h:h + 1], scale=-1.0)
                if k == 1:
                    last.then_inc(D_ok, 1)

            def high_scores(n):
                act.wait_ge(C_ok, 2 * n + 2)
                if n >= 2:
                    act.wait_ge(pv_ok, n - 1)
                act.activation(Chi[:, n % 2], Z[:, n % 3], ACT.Copy).then_inc(Chi_ok, 1)

            def squares(b):
                act.wait_ge(hm_ok, b + 1)
                act.activation(hsq[:, b % 2], hm[:, b % 2], ACT.Square).then_inc(hsq_ok, 1)

            def high_rows(b):
                act.wait_ge(nb2_ok, b + 1)
                if b >= 2:
                    act.wait_ge(x2_low, b - 1)
                    act.wait_ge(*x2_bank(b - 2)[1:])
                link(act.activation(x2[:, b % 2, :], x1[:, b, :], ACT.Identity, bias=nb[:, B + b:B + b + 1],
                                    scale=rstd[:, B + b:B + b + 1]))
                act.activation(x2hl[:, b % 2, 0, :], x2[:, b % 2, :], ACT.Copy).then_inc(x2_hi, 1)

            def x2_columns(b):
                source, full, count = x2_bank(b)
                g, r = group_of(b)
                act.wait_ge(full, count)
                if g >= 2:
                    act.wait_ge(up_ok, SLOTS * (g - 1))
                o = x2T[:, g % 2, :, :, r * S:(r + 1) * S].rearrange("p a k s -> p (a k) s")
                act.activation(o, source[:, 0:4 * S].rearrange("p (k s) -> p k s", k=4), ACT.Copy).then_inc(x2T_ok, 1)

            def route_exps(g):
                act.wait_ge(nmx_ok, g + 1)
                for b in range(size(g)):
                    act.activation(ex[:, g % 2, b, 0:NEX], lg[:, g % 2, b, 0:NEX], ACT.Exp,
                                   bias=nmx[:, g % 2, b:b + 1], accum_out=esum[:, g % 2, b, 0:1]).then_inc(ex_ok, 1)
                    act.activation(ex[:, g % 2, b, NEX:NEX + 1], lg[:, g % 2, b, NEX:NEX + 1], ACT.Exp,
                                   scale=-1.0).then_inc(ex_ok, 1)

            def route_columns(g):
                act.wait_ge(M_full, M_AT["route_cols", g])
                if g >= 2:
                    act.wait_ge(*spread_bank(g - 2, SPREADS - 1)[1:])
                n = size(g) * S
                act.activation(cT[:, g % 2, 0:n], pM16[0:2 * NEX, 0:n], ACT.Copy).then_inc(cT_ok, 1)

            def spread_out(g, i):
                for j in range(2 * i, 2 * i + 2):
                    f0, f1 = 2 * j, min(2 * j + 2, NC_EX)
                    source, full, count = spread_bank(g, j)
                    act.wait_ge(full, count)
                    if g >= 1:
                        act.wait_ge(h_ok, SLOTS * (g - 1) + NC_SH + f1)
                    n = size(g) * S
                    weights = source[:, :].rearrange("p (f t) -> p f t", t=TOK)
                    act.activation(cw[:, f0:f1, 0:n], weights[:, 0:f1 - f0, 0:n], ACT.Copy).then_inc(cw_ok, 1)

            def high_weights(c):
                p = part(c)
                act.wait_ge(wmul_ok, p + 1)
                w = 1 if c == PAIRED else 2
                act.activation(up16[:, c, 0, 0:w], w_up[:, c, 0:w], ACT.Copy, scale=wmul[:, p:p + 1]).then_inc(whi_ok, 1)

            def gate_tanh(n):
                g, c = divmod(n, SLOTS)
                f1, tok = gate_rows_of(c), size(g) * S
                act.wait_ge(up_ok, n + 1)
                if n >= 2:
                    act.wait_ge(h_ok, n - 1)
                act.activation(s_ff[f1, n % 2, 0:tok], pU[n % 2][f1, 0:tok], ACT.Tanh,
                               scale=unscale[f1, part(c), 0:1]).then_inc(s_ok, 1)

            for t in range(END):
                if (n := chunk_at(t, ACT_AT["tanh"])) is not None:
                    gate_tanh(n)
                for i in range(3):
                    if (g := late_at(t, ACT_AT["spread"][i])) is not None:
                        spread_out(g, i)
                for b in range(GB):
                    if (g := group_at(t, ACT_AT["queries"][b], b + 1)) is not None:
                        query_columns(FIRST[g] + b)
                    if (g := group_at(t, ACT_AT["keys"][b], b + 1)) is not None:
                        key_columns(FIRST[g] + b)
                if (g := group_at(t, ACT_AT["gate_cols"])) is not None:
                    gate_columns(g)
                for b in range(GB):
                    if (g := late_at(t, ACT_AT["x2_cols"][b], b + 1)) is not None:
                        x2_columns(FIRST[g] + b)
                if (g := late_at(t, ACT_AT["route"])) is not None:
                    route_exps(g)
                if (g := late_at(t, ACT_AT["route_cols"])) is not None:
                    route_columns(g)
                for b in range(GB):
                    if (g := late_at(t, ACT_AT["squares"][b], b + 1)) is not None:
                        squares(FIRST[g] + b)
                    if (g := late_at(t, ACT_AT["x2"][b], b + 1)) is not None:
                        high_rows(FIRST[g] + b)
                if (g := group_at(t, ACT_AT["forget"])) is not None:
                    forget_logs(g)
                for u in range(GB * UNITS):
                    if (g := group_at(t, ACT_AT["high"][u], u // UNITS + 1)) is not None:
                        high_scores(UNITS * FIRST[g] + u)
                    for i in range(2):
                        if (g := group_at(t, ACT_AT["decays"][2 * u + i], u // UNITS + 1)) is not None:
                            decays(UNITS * FIRST[g] + u, i)
                if (g := group_at(t, ACT_AT["key_parts"])) is not None:
                    high_keys(g)
                if (g := group_at(t, ACT_AT["query_parts"])) is not None:
                    high_queries(g)
                for c in range(SLOTS):
                    if t == SPLIT[c]:
                        high_weights(c)

        @block.vector
        def _(dve):
            steps = [0]

            def link(instruction):
                steps[0] += 1
                instruction.then_inc(dve_step, 1)
                dve.wait_ge(dve_step, steps[0])

            def gate_weights():
                dve.wait_ge(in_wg, 32)
                wi = wg_in[:, :, :].rearrange("p w (j n) -> p w j n", j=NPAIR)
                link(dve.tensor_tensor(wi[:, 1], wi[:, 1], wi[:, 2], ALU.add))
                link(dve.tensor_copy(wg_sb[:, :, :, 0, :], wi[:, 0:2]))
                link(dve.tensor_tensor(wg_r[:, :, :, :], wi[:, 0:2], wg_sb[:, :, :, 0, :], ALU.subtract))
                link(dve.tensor_copy(wg_sb[:, :, :, 1, :], wg_r[:, :, :, :]))
                dve.tensor_tensor(wg_sb[:, :, :, 2, :], wg_r[:, :, :, :], wg_sb[:, :, :, 1, :], ALU.subtract)\
                    .then_inc(wg_part, 1)

            def route_weights():
                dve.wait_ge(in_late, 64)
                link(dve.tensor_copy(gw3[:, :, 0, :], gw[:, :, :]))
                link(dve.tensor_tensor(gwr[:, :, :], gw[:, :, :], gw3[:, :, 0, :], ALU.subtract))
                link(dve.tensor_copy(gw3[:, :, 1, :], gwr[:, :, :]))
                dve.tensor_tensor(gw3[:, :, 2, :], gwr[:, :, :], gw3[:, :, 1, :], ALU.subtract).then_inc(gw_ok, 1)

            def weight_sizes(p, i):
                c0, c1 = piece(p, i)
                dve.wait_ge(in_up[p][i], 16)
                dve.tensor_reduce(wmax[:, p, i:i + 1], w_up[:, c0:c1].rearrange("p c w k f -> p (c w k f)"), AX.X,
                                  ALU.max, apply_absolute_value=True).then_inc(wmax_ok, 1)

            def weight_scales(p):
                dve.wait_ge(wall_ok, p + 1)
                link(dve.tensor_reduce(wpow[:, p, 1:2], wall[:, p, :], AX.X, ALU.max))
                link(dve.tensor_scalar(wpow[:, p, 1:2], wpow[:, p, 1:2], 1e-30, None, ALU.max))
                link(dve.tensor_scalar(wpow[:, p, 0:1].bitcast(I32), wpow[:, p, 1:2].bitcast(I32), 0x7F800000, None,
                                       ALU.bitwise_and))
                link(dve.reciprocal(wpow[:, p, 1:2], wpow[:, p, 0:1]))
                link(dve.tensor_scalar(unscale[:, p, 0:1], wpow[:, p, 0:1], 0.5 / UPSCALE, None, ALU.mult))
                link(dve.tensor_scalar(unscale[:, p, 1:2], unscale[:, p, 0:1], unscale[:, p, 0:1], 2 / (1, WSCALE)[p],
                                       ALU.mult, ALU.mult))
                dve.tensor_scalar(wmul[:, p:p + 1], wpow[:, p, 1:2], MSCALE, None, ALU.mult).then_inc(wmul_ok, 1)

            def low_weights(c):
                p = part(c)
                dve.wait_ge(whi_ok, c + 1)
                w = 1 if c == PAIRED else 2
                dve.scalar_tensor_tensor(out=up16[:, c, 1, 0:w].rearrange("p w k f -> p (w k f)"),
                                         in0=w_up[:, c, 0:w].rearrange("p w k f -> p (w k f)"), scalar=wmul[:, p:p + 1],
                                         in1=up16[:, c, 0, 0:w].rearrange("p w k f -> p (w k f)"),
                                         op0=ALU.mult, op1=ALU.subtract).then_inc(wlo_ok, 1)

            def row_stats(g):
                for b in rows_of(g):
                    dve.wait_ge(in_rows[b], 32)
                    steps[0] += 1
                    dve.bn_stats(st6[:, b, :], x_sb[:, b, :]).then_inc(dve_step, 1)
                steps[0] += 1
                dve.tensor_reduce(kmax[:, g:g + 1], ctx_sb[:, FIRST[g]:FIRST[g + 1], :].rearrange("p b e -> p (b e)"), AX.X,
                                  ALU.max, apply_absolute_value=True).then_inc(dve_step, 1)
                dve.wait_ge(dve_step, steps[0])
                for b in rows_of(g):
                    last = dve.bn_aggr(mv[:, b, :], st6[:, b, :])
                last.then_inc(stats_ok, 1)

            def row_scales(g):
                dve.wait_ge(rstd_ok, 2 * g + 2)
                n = slice(FIRST[g], FIRST[g + 1])
                link(dve.tensor_scalar(kall[:, g:g + 1], kall[:, g:g + 1], 1e-30, None, ALU.max))
                link(dve.tensor_scalar(kpow[:, g, 0:1].bitcast(I32), kall[:, g:g + 1].bitcast(I32), 0x7F800000, None,
                                       ALU.bitwise_and))
                link(dve.reciprocal(kpow[:, g, 1:2], kpow[:, g, 0:1]))
                dve.tensor_scalar(kpow[:, g, 2:3], kpow[:, g, 1:2], KSCALE, None, ALU.mult)
                link(dve.tensor_scalar(kpow[:, g, 3:4], kpow[:, g, 0:1], 1 / KSCALE, None, ALU.mult))
                dve.tensor_scalar(kpow[:, g, 4:5], kpow[:, g, 3:4], RSUM, None, ALU.mult)
                link(dve.tensor_scalar(kpow[:, g, 5:6], kpow[:, g, 3:4], kpow[:, g, 3:4], RSUM, ALU.mult, ALU.mult))
                dve.scalar_tensor_tensor(out=nb[:, n], in0=mv[:, n, 0], scalar=-1.0, in1=rstd[:, n],
                                         op0=ALU.mult, op1=ALU.mult).then_inc(scales_ok, 1)

            def low_keys(g):
                for b in rows_of(g):
                    dve.wait_ge(k_hi, b + 1)
                    c = ctx_sb[:, b, :].rearrange("p (h i) -> p h i", i=DH)
                    dve.scalar_tensor_tensor(out=k3[:, b % 4, :, 1, :], in0=c, scalar=kpow[:, g, 2:3],
                                             in1=k3[:, b % 4, :, 0, :], op0=ALU.mult, op1=ALU.subtract)\
                        .then_inc(k_low, 1)

            def gates(b):
                g, r = group_of(b)
                source, full, count = gates_bank(b)
                dve.wait_ge(full, count)
                dve.tensor_reduce(gred[:, r], source[:, 0:192].rearrange("p (a s i) -> p a i s", a=2, s=3),
                                  AX.X, ALU.add).then_inc(gsum_ok, 1)
                dve.wait_ge(gsum_ok, b + 1)
                link(dve.scalar_tensor_tensor(out=gt1[:, r, :], in0=gred[:, r, 1, :], scalar=kpow[:, g, 3:4],
                                              in1=bias_sb[:, :], op0=ALU.mult, op1=ALU.add))
                if g >= 2:
                    dve.wait_ge(T_full, T_AT["gate_rows", g - 2])
                dve.scalar_tensor_tensor(out=g_tm[:, g % 2, :, r, :],
                                         in0=gred[:, r, 0, :].rearrange("p (a h) -> p a h", a=2),
                                         scalar=1.0 / QSCALE, in1=gt1[:, r, :].rearrange("p (a h) -> p a h", a=2),
                                         op0=ALU.mult, op1=ALU.add).then_inc(gates_ok, 1)

            def gate_rows(g):
                dve.wait_ge(T_full, T_AT["gate_rows", g])
                m = size(g) * NH
                dve.tensor_copy(gT[0:m, :, :], pT[0:m, 0:2 * S].rearrange("p (a s) -> p a s", a=2))\
                    .then_inc(gT_ok, 1)

            def gate_scans(g):
                dve.wait_ge(gln_ok, g + 1)
                dve.wait_ge(gT_ok, g + 1)
                m = size(g) * NH
                link(dve.scalar_tensor_tensor(out=lf[0:m, 0, :], in0=gT[0:m, 1, :], scalar=0.0, in1=gabs[0:m, 2, :],
                                              op0=ALU.min, op1=ALU.subtract))
                link(dve.tensor_tensor_scan(lf[0:m, 1, :], ones[0:m, :], lf[0:m, 0, :], 0.0, ALU.mult, ALU.add))
                if g >= 1:
                    dve.wait_ge(M_full, M_AT["gate_cols", g - 1])
                if g >= 2:
                    dve.wait_ge(g_row_in, 16 * (g - 1))
                link(dve.tensor_tensor(aM[0:m, 0, :], gT[0:m, 0, :], lf[0:m, 1, :], ALU.subtract))
                link(dve.tensor_tensor_scan(Gm[0:m, g % 2, :], aM[0:m, 0, :], aM[0:m, 0, :], -3e38, ALU.max, ALU.max))
                dve.tensor_tensor(aM[0:m, 1, :], lf[0:m, 1, :], Gm[0:m, g % 2, :], ALU.add).then_inc(aM_ok, 1)

            def scores(n):
                dve.wait_ge(D_ok, n + 1)
                z = Z[:, n % 3].rearrange("p (j e) s -> p j e s", e=2)
                for e in range(2):
                    dve.wait_ge(qk_ok, 2 * n + e + 1)
                    dve.scalar_tensor_tensor(out=z[:, :, e, :], in0=pQK[e][:, :].rearrange("p (j s) -> p j s", s=S),
                                             scalar=CSCALE, in1=z[:, :, e, :], op0=ALU.mult, op1=ALU.mult)\
                        .then_inc(C_ok, 1)

            def head_sums(n):
                dve.wait_ge(pv_ok, n + 1)
                r, h0 = (n // 2) % 2, (n % 2) * UH
                pv = pPV[:, :].rearrange("p (h w) -> p h w", w=64)
                dve.tensor_reduce(U[:, r, h0:h0 + UH, :], pv[:, :, 0:2 * DH].rearrange("p h (s i) -> p h i s", s=2),
                                  AX.X, ALU.add)
                dve.tensor_copy(rs[:, r, h0:h0 + UH], pv[:, :, 3 * DH]).then_inc(pv_used, 1)

            def normalizers(b):
                g, place = group_of(b)
                r = b % 2
                dve.wait_ge(eM_ok, g + 1)
                dve.wait_ge(pv_used, 2 * b + 2)
                n = nrm[:, r]
                link(dve.scalar_tensor_tensor(out=n[:, 0, :], in0=rs[:, r, :], scalar=-1.0, in1=rs[:, r, :],
                                              op0=ALU.mult, op1=ALU.max))
                link(dve.scalar_tensor_tensor(out=n[:, 1, :], in0=n[:, 0, :], scalar=kpow[:, g, 4:5],
                                              in1=eM[:, g % 2, place * NH:(place + 1) * NH], op0=ALU.mult, op1=ALU.max))
                link(dve.tensor_scalar(n[:, 2, :], n[:, 1, :], EPS, None, ALU.add))
                link(dve.reciprocal(n[:, 3, :], n[:, 2, :]))
                steps[0] += 1
                dve.tensor_scalar(n[:, 4, :], n[:, 3, :], kpow[:, g, 5:6], None, ALU.mult).then_inc(dve_step, 1)

            def head_means(b):
                r = b % 2
                n = nrm[:, r]
                dve.wait_ge(dve_step, steps[0])
                link(dve.tensor_tensor(hh[:, :, :], U[:, r], bc(n[:, 4, :], DH), ALU.mult))
                link(dve.tensor_reduce(hst[:, r, 0, :], hh[:, :, :], AX.X, ALU.add))
                dve.scalar_tensor_tensor(out=hm[:, r], in0=bc(hst[:, r, 0, :], DH), scalar=-1.0 / DH,
                                         in1=hh[:, :, :], op0=ALU.mult, op1=ALU.add).then_inc(hm_ok, 1)

            def head_variances(b):
                r = b % 2
                dve.wait_ge(hsq_ok, b + 1)
                dve.tensor_reduce(hst[:, r, 1, :], hsq[:, r], AX.X, ALU.add).then_inc(hvar_ok, 1)

            def residual(b):
                dve.wait_ge(ho_ok, b + 1)
                link(dve.tensor_tensor(x1[:, b, :], x_sb[:, b, :], hsq[:, b % 2].rearrange("p h i -> p (h i)"), ALU.add))
                link(dve.bn_stats(st6[:, B + b, :], x1[:, b, :]))
                dve.bn_aggr(mv[:, B + b, :], st6[:, B + b, :]).then_inc(stats2_ok, 1)

            def row_offset(b):
                n = slice(B + b, B + b + 1)
                dve.wait_ge(rstd2_ok, b + 1)
                dve.scalar_tensor_tensor(out=nb[:, n], in0=mv[:, n, 0], scalar=-1.0, in1=rstd[:, n],
                                         op0=ALU.mult, op1=ALU.mult).then_inc(nb2_ok, 1)

            def route(g):
                r, m = g % 2, size(g)
                dve.wait_ge(M_full, M_AT["logits", g])
                dve.tensor_reduce(lgs[:, r, 0:m], pM[:, 0:128].rearrange("p (b w) -> p b w", b=GB)[:, 0:m, 0:3 * (NEX + 1)]
                                  .rearrange("p b (s e) -> p b e s", s=3), AX.X, ALU.add).then_inc(lgs_ok, 1)
                dve.wait_ge(lgs_ok, g + 1)
                link(dve.tensor_scalar(lg[:, r, 0:m], lgs[:, r, 0:m], 1 / QSCALE, None, ALU.mult))
                l = lg[:, r, 0:m, 0:NEX]
                dve.tensor_reduce(nmx[:, r, 0:m], l, AX.X, ALU.max, negate=True).then_inc(nmx_ok, 1)

            def ranks(g):
                r, m = g % 2, size(g)
                l = lg[:, r, 0:m, 0:NEX]
                dve.wait_ge(nmx_ok, g + 1)
                gt, eq, beat = (cmpt[:, i, 0:m].rearrange("p b (e j) -> p b e j", j=NEX) for i in range(3))
                for b in range(m):
                    lj = l[:, b, :].unsqueeze(1).to_broadcast([P, NEX, NEX])
                    le = l[:, b, :].unsqueeze(2).to_broadcast([P, NEX, NEX])
                    dve.tensor_tensor(gt[:, b], lj, le, ALU.is_gt)
                    link(dve.tensor_tensor(eq[:, b], lj, le, ALU.is_equal))
                for b in range(m):
                    last = dve.tensor_tensor(beat[:, b], eq[:, b], low[:, :, :], ALU.mult)
                link(last)
                link(dve.tensor_tensor(gt, gt, beat, ALU.add))
                dve.tensor_reduce(rank[:, r, 0, 0:m], gt, AX.X, ALU.add)

            def route_part2(g):
                r, m = g % 2, size(g)
                dve.wait_ge(ex_ok, 2 * FIRST[g + 1])
                link(dve.tensor_scalar(esum[:, r, 0:m, 1], ex[:, r, 0:m, NEX], 1.0, None, ALU.add))
                link(dve.reciprocal(rcp[:, r, 0:m], esum[:, r, 0:m]))
                link(dve.scalar_tensor_tensor(out=rank[:, r, 1, 0:m], in0=rank[:, r, 0, 0:m], scalar=2.0,
                                              in1=ex[:, r, 0:m, 0:NEX], op0=ALU.is_lt, op1=ALU.mult))
                for b in range(m):
                    last = dve.tensor_scalar(rank[:, r, 0, b, :], rank[:, r, 1, b, :], rcp[:, r, b, 0:1], WSCALE,
                                             ALU.mult, ALU.mult)
                link(last)
                if g >= 2:
                    dve.wait_ge(M_full, M_AT["route_cols", g - 2])
                link(dve.tensor_copy(c16[:, r, 0:m, 0, :], rank[:, r, 0, 0:m]))
                dve.tensor_tensor(c16[:, r, 0:m, 1, :], rank[:, r, 0, 0:m], c16[:, r, 0:m, 0, :], ALU.subtract)\
                    .then_inc(c16_ok, 1)

            def features(n):
                g, c = divmod(n, SLOTS)
                f1, f2, tok = gate_rows_of(c), rows_in(c), size(g) * S
                at2 = 0 if c == PAIRED else TOK
                up1, up2 = pU[n % 2][f1, 0:tok], pU[n % 2][f2, at2:at2 + tok]
                t, p, h = s_ff[f1, n % 2, 0:tok], p_ff[f2, n % 2, 0:tok], h_ff[f2, n % 3, 0:tok]
                factor = unscale[f2, part(c), 1:2]
                dve.wait_ge(s_ok, n + 1)
                if c < NC_SH:
                    link(dve.scalar_tensor_tensor(out=p, in0=t, scalar=1.0, in1=up1, op0=ALU.add, op1=ALU.mult))
                else:
                    f = c - NC_SH
                    dve.wait_ge(cw_ok, SPREADS * g + f // 2 + 1)
                    link(dve.scalar_tensor_tensor(out=p, in0=t, scalar=1.0, in1=cw[:, f, 0:tok], op0=ALU.add, op1=ALU.mult))
                    link(dve.tensor_tensor(p, p, up1, ALU.mult))
                if n >= 3:
                    dve.wait_ge(dn_used, n - 2)
                dve.scalar_tensor_tensor(out=h, in0=p, scalar=factor, in1=up2, op0=ALU.mult, op1=ALU.mult)\
                    .then_inc(h_ok, 1)

            def shared_out(g):
                dve.wait_ge(dn_used, SLOTS * g + NC_SH)
                for b in range(size(g)):
                    n = FIRST[g] + b
                    dve.scalar_tensor_tensor(out=y_sb[:, n, :], in0=pD[:, b * E:(b + 1) * E],
                                             scalar=rcp[:, g % 2, b, 1:2], in1=x1[:, n, :],
                                             op0=ALU.mult, op1=ALU.add).then_inc(y_ok, 1)

            def final_out(g):
                dve.wait_ge(dn_used, SLOTS * (g + 1))
                dve.wait_ge(y_ok, FIRST[g + 1])
                for b in range(size(g)):
                    n = FIRST[g] + b
                    dve.tensor_tensor(o_sb[:, n, :], y_sb[:, n, :], pD[:, b * E:(b + 1) * E], ALU.add).then_inc(o_ok, 1)

            dve.wait_ge(pool_const, 5)
            for t in range(END):
                if (g := group_at(t, DVE_AT["stats"])) is not None:
                    row_stats(g)
                if t == ONCE["gate_weights"]:
                    gate_weights()
                if t == ONCE["route_weights"]:
                    route_weights()
                if (g := late_at(t, DVE_AT["shared"])) is not None:
                    shared_out(g)
                if (g := late_at(t, DVE_AT["final"])) is not None:
                    final_out(g)
                if (g := group_at(t, DVE_AT["scales"])) is not None:
                    row_scales(g)
                if (g := group_at(t, DVE_AT["key_parts"])) is not None:
                    low_keys(g)
                for b in range(GB):
                    if (g := group_at(t, DVE_AT["gates"][b], b + 1)) is not None:
                        gates(FIRST[g] + b)
                if (g := group_at(t, DVE_AT["gate_rows"])) is not None:
                    gate_rows(g)
                if (g := group_at(t, DVE_AT["scans"])) is not None:
                    gate_scans(g)
                for u in range(GB * UNITS):
                    if (g := group_at(t, DVE_AT["sums"][u], u // UNITS + 1)) is not None:
                        head_sums(UNITS * FIRST[g] + u)
                    if (g := group_at(t, DVE_AT["scores"][u], u // UNITS + 1)) is not None:
                        scores(UNITS * FIRST[g] + u)
                for b in range(GB):
                    if (g := late_at(t, DVE_AT["norms"][b], b + 1)) is not None:
                        normalizers(FIRST[g] + b)
                    if (g := late_at(t, DVE_AT["means"][b], b + 1)) is not None:
                        head_means(FIRST[g] + b)
                    if (g := late_at(t, DVE_AT["variances"][b], b + 1)) is not None:
                        head_variances(FIRST[g] + b)
                    if (g := late_at(t, DVE_AT["residual"][b], b + 1)) is not None:
                        residual(FIRST[g] + b)
                    if (g := late_at(t, DVE_AT["offset"][b], b + 1)) is not None:
                        row_offset(FIRST[g] + b)
                if (g := late_at(t, DVE_AT["route"])) is not None:
                    route(g)
                if (g := late_at(t, DVE_AT["ranks"])) is not None:
                    ranks(g)
                if (g := late_at(t, DVE_AT["route2"])) is not None:
                    route_part2(g)
                for p in range(2):
                    for i in range(PIECES):
                        if t == SIZES[p][i]:
                            weight_sizes(p, i)
                    if t == WSCALES[p]:
                        weight_scales(p)
                for c in range(SLOTS):
                    if t == SPLIT[c] + 1:
                        low_weights(c)
                if (n := chunk_at(t, DVE_AT["features"])) is not None:
                    features(n)

        @block.tensor
        def _(pe):
            read = {"keys": kT_ok, "queries": qT_ok, "gates": gsum_ok, "gate_rows": gT_ok, "gate_cols": eM_ok, "x2_cols": x2T_ok,
                    "logits": lgs_ok, "route_cols": cT_ok, "spread": cw_ok}
            units = [0]

            def free(before, key):
                if before[key] is not None:
                    name, n = before[key]
                    pe.wait_ge(read[name], n + 1)

            def score_bank_free(e):
                if units[0]:
                    pe.wait_ge(C_ok, 2 * (units[0] - 1) + e + 1)

            def columns(source, o):
                for j in range(NPAIR):
                    last = pe.transpose(o[:, j * S:(j + 1) * S], source[:, 2 * j:2 * j + 2].rearrange("p h s i -> p (h s i)"),
                                        id16[:, :])
                return last

            def key_columns(b):
                free(T_BEFORE, ("keys", b))
                pe.wait_ge(k_low, b + 1)
                columns(k3[:, b % 4], pT16).then_inc(T_full, 1)

            def query_columns(b):
                free(M_BEFORE, ("queries", b))
                pe.wait_ge(q_low, b + 1)
                columns(q3[:, b % 2], pM16).then_inc(M_full, 1)

            def gates(b):
                o, full, _ = gates_bank(b)
                free((T_BEFORE, M_BEFORE)[group_of(b)[1]], ("gates", b))
                pe.wait_ge(qT_ok, b + 1)
                pe.wait_ge(kT_ok, b + 1)
                pe.wait_ge(wg_part, 1)
                for w, operand in enumerate((qT, kT)):
                    for j in range(NPAIR):
                        last = pe.matmul(o[:, 96 * w:96 * w + 96], operand[:, b % 4, j, :],
                                         wg_sb[:, w, j].rearrange("p s n -> p (s n)"),
                                         start=(j == 0), stop=(j == NPAIR - 1))
                last.then_inc(full, 1)

            def gate_rows(g):
                free(T_BEFORE, ("gate_rows", g))
                pe.wait_ge(gates_ok, FIRST[g + 1])
                for a in range(2):
                    last = pe.transpose(pT[0:size(g) * NH, a * S:(a + 1) * S],
                                        g_tm[:, g % 2, a, 0:size(g)].rearrange("p b h -> p (b h)"), id32[:, :])
                last.then_inc(T_full, 1)

            def gate_columns(g):
                free(M_BEFORE, ("gate_cols", g))
                pe.wait_ge(aM_ok, g + 1)
                for a in range(2):
                    m = size(g) * NH
                    last = pe.transpose(pM[:, 64 * a:64 * a + m], aM[0:m, a, :], id32[0:m, 0:m])
                last.then_inc(M_full, 1)

            def scores(n):
                b, h0 = n // 2, (n % 2) * UH
                for e in range(2):
                    score_bank_free(e)
                    for i in range(UH // 2):
                        j, base = (h0 + 2 * i) // 2, 64 * e
                        last = pe.matmul(pQK[e][:, i * S:(i + 1) * S], kT[base:base + 3 * DH, b % 4, j, :],
                                         qT[base:base + 3 * DH, b % 4, j, :], start=True, stop=True)
                    last.then_inc(qk_ok, 1)
                units[0] += 1

            def outputs(n):
                b, h0 = n // 2, (n % 2) * UH
                pe.wait_ge(Clo_ok, n + 1)
                if n >= 1:
                    pe.wait_ge(pv_used, n)
                for i in range(UH):
                    o = pPV[:, 64 * i:64 * i + 3 * DH + 1]
                    v = k3[:, b % 4, h0 + i].rearrange("p s i -> p (s i)")[:, 0:3 * DH + 1]
                    pe.matmul(o, Chi[:, n % 2, i, :], v, start=True, stop=False)
                    last = pe.matmul(o, Clo[:, n % 2, i, :], v, start=False, stop=True)
                last.then_inc(pv_ok, 1)

            def x2_columns(b):
                o, full, _ = x2_bank(b)
                free((T_BEFORE, M_BEFORE)[group_of(b)[1]], ("x2_cols", b))
                pe.wait_ge(x2_low, b + 1)
                for i in range(4):
                    last = pe.transpose(o[:, i * S:(i + 1) * S],
                                        x2hl[:, b % 2, i // 2, (i % 2) * P:(i % 2 + 1) * P], id16[:, :])
                last.then_inc(full, 1)

            def logits(g):
                free(M_BEFORE, ("logits", g))
                pe.wait_ge(x2T_ok, FIRST[g + 1])
                pe.wait_ge(gw_ok, 1)
                for b in range(size(g)):
                    for i in range(4):
                        last = pe.matmul(pM[:, 64 * b:64 * b + 3 * (NEX + 1)],
                                         x2T[:, g % 2, i // 2, i % 2, b * S:(b + 1) * S],
                                         gw3[:, i % 2].rearrange("p s e -> p (s e)"), start=(i == 0), stop=(i == 3))
                last.then_inc(M_full, 1)

            def route_columns(g):
                free(M_BEFORE, ("route_cols", g))
                pe.wait_ge(c16_ok, g + 1)
                for b in range(size(g)):
                    last = pe.transpose(pM16[0:2 * NEX, b * S:(b + 1) * S],
                                        c16[:, g % 2, b].rearrange("p s e -> p (s e)"), id16[:, :])
                last.then_inc(M_full, 1)

            def spread(g, i):
                pe.wait_ge(cT_ok, g + 1)
                if g == 0 and i == 0:
                    pe.wait_ge(in_late, 64)
                for j in range(2 * i, 2 * i + 2):
                    o, full, _ = spread_bank(g, j)
                    free((T_BEFORE, M_BEFORE)[j % 2], ("spread", SPREADS * g + j))
                    for f in range(2 * j, min(2 * j + 2, NC_EX)):
                        n = size(g) * S
                        last = pe.matmul(o[:, (f % 2) * TOK:(f % 2) * TOK + n], sel[:, f * P:(f + 1) * P],
                                         cT[:, g % 2, 0:n], start=True, stop=True)
                    last.then_inc(full, 1)

            def expert_up(n):
                g, c = divmod(n, SLOTS)
                tok = size(g) * S
                if c == 0:
                    pe.wait_ge(x2T_ok, FIRST[g + 1])
                if g == 0:
                    pe.wait_ge(wlo_ok, c + 1)
                if n >= 2:
                    pe.wait_ge(h_ok, n - 1)
                for w in range(1 if c == PAIRED else 2):
                    for kk in range(2):
                        for i, (a, part_x) in enumerate(((0, 0), (0, 1), (1, 0))):
                            last = pe.matmul(pU[n % 2][:, w * TOK:w * TOK + tok], up16[:, c, a, w, kk, :],
                                             x2T[:, g % 2, part_x, kk, 0:tok], start=(kk == 0 and i == 0),
                                             stop=(kk == 1 and i == 2))
                last.then_inc(up_ok, 1)

            def expert_down(n):
                g, c = divmod(n, SLOTS)
                f2 = rows_in(c)
                if g == 0 and c in (0, NC_SH):
                    pe.wait_ge(in_dn[part(c)], 16)
                if c == 0 and g > 0:
                    pe.wait_ge(o_ok, FIRST[g])
                if c == NC_SH:
                    pe.wait_ge(y_ok, FIRST[g + 1])
                pe.wait_ge(h_ok, n + 1)
                for b in range(size(g)):
                    last = pe.matmul(pD[:, b * E:(b + 1) * E], h_ff[f2, n % 3, b * S:(b + 1) * S],
                                     w_dn[f2, c, :], start=(b == 0 and c in (0, NC_SH)),
                                     stop=c in (NC_SH - 1, SLOTS - 1), skip_group_check=True)
                last.then_inc(dn_used, 1)

            pe.wait_ge(in_const, 32)
            pe.wait_ge(pool_const, 5)
            for t in range(END):
                for b in range(GB):
                    if (g := group_at(t, PE_AT["queries"][b], b + 1)) is not None:
                        query_columns(FIRST[g] + b)
                    if (g := group_at(t, PE_AT["gates"][b], b + 1)) is not None:
                        gates(FIRST[g] + b)
                    if (g := group_at(t, PE_AT["keys"][b], b + 1)) is not None:
                        key_columns(FIRST[g] + b)
                if (g := group_at(t, PE_AT["gate_rows"])) is not None:
                    gate_rows(g)
                if (g := group_at(t, PE_AT["gate_cols"])) is not None:
                    gate_columns(g)
                for u in range(GB * UNITS):
                    if (g := group_at(t, PE_AT["scores"][u], u // UNITS + 1)) is not None:
                        scores(UNITS * FIRST[g] + u)
                    if (g := group_at(t, PE_AT["outputs"][u], u // UNITS + 1)) is not None:
                        outputs(UNITS * FIRST[g] + u)
                for b in range(GB):
                    if (g := late_at(t, PE_AT["x2_cols"][b], b + 1)) is not None:
                        x2_columns(FIRST[g] + b)
                if (g := late_at(t, PE_AT["logits"])) is not None:
                    logits(g)
                if (g := late_at(t, PE_AT["route_cols"])) is not None:
                    route_columns(g)
                for i in range(3):
                    if (g := late_at(t, PE_AT["spread"][i])) is not None:
                        spread(g, i)
                if (n := chunk_at(t, PE_AT["up"])) is not None:
                    expert_up(n)
                if (n := chunk_at(t, PE_AT["down"])) is not None:
                    expert_down(n)


def constants():
    ident = np.eye(P, dtype=np.float32)
    expert = np.arange(NC_EX * P) // FM
    select = (np.arange(2 * NEX)[:, None] % NEX == expert[None, :]).astype(np.float16)
    lower = np.broadcast_to(np.tril(np.ones((NEX, NEX), np.float32), -1), (P, NEX, NEX))
    return {"ident": ident, "ident16": ident.astype(np.float16), "select": select,
            "lower": np.ascontiguousarray(lower)}


def layouts(a):
    out = {"x": a["x"], "ctx_in": a["ctx_2048"]}
    gates = np.concatenate([a["L0_xattn_Wi"], a["L0_xattn_Wf"]], axis=1)
    gates = gates.reshape(3, NPAIR, 2, DH, 2 * NH).transpose(0, 2, 3, 1, 4)
    wg = np.zeros((2, 4, DH, 3, NPAIR, 2 * NH), np.float32)
    for slot in (0, 2):
        wg[:, slot, :, 0] = gates[0]
    for w in (1, 2):
        for slot in (0, 1):
            wg[:, slot, :, w] = gates[w]
    out["wg"] = wg.reshape(P, 3, NPAIR * 2 * NH)
    out["bias_g"] = np.concatenate([a["L0_xattn_bi"], a["L0_xattn_bf"]])
    out["ln_scale"] = a["L0_xattn_ln_scale"]
    route = np.concatenate([a["L0_ffn_gate_w"], a["L0_ffn_shared_gate_w"]], axis=0)
    out["gate_w"] = route.T.reshape(2, P, NEX + 1).transpose(1, 0, 2)
    up = np.zeros((2, SLOTS * P, E), np.float32)
    for w in range(2):
        whole = PAIRED * P
        up[w, 0:whole] = a[f"L0_ffn_shared_fc{w + 1}"][0:whole]
        up[0, whole + w * REST:whole + (w + 1) * REST] = a[f"L0_ffn_shared_fc{w + 1}"][whole:]
        up[w, NC_SH * P:] = a[f"L0_ffn_expert_fc{w + 1}"].reshape(NEX * FM, E)
    out["up"] = up.reshape(2, SLOTS, P, 2, P).transpose(1, 4, 0, 3, 2)
    down = np.zeros((SLOTS * P, E), np.float32)
    down[0:whole] = a["L0_ffn_shared_proj"].T[0:whole]
    down[whole + REST:NC_SH * P] = a["L0_ffn_shared_proj"].T[whole:]
    down[NC_SH * P:] = a["L0_ffn_expert_proj"].transpose(0, 2, 1).reshape(NEX * FM, E)
    out["down"] = down.reshape(SLOTS, P, E).transpose(1, 0, 2)
    return {k: np.ascontiguousarray(v) for k, v in out.items()}


def kernel(**inputs):
    import concourse.bacc as bacc
    from concourse.bass_utils import run_bass_kernel_spmd

    arrays = layouts({k: np.asarray(v) for k, v in inputs.items()}) | constants()
    nc = bacc.Bacc("TRN2", target_bir_lowering=False, num_devices=1)
    args = {k: nc.dram_tensor(k, v.shape, mybir.dt.from_np(v.dtype), kind="ExternalInput").ap()
            for k, v in arrays.items()}
    out = nc.dram_tensor("out", (B, S, E), F32, kind="ExternalOutput").ap()
    build(nc, **args, out=out)
    r = run_bass_kernel_spmd(nc, [arrays], core_ids=[0])
    return r.results[0]["out"]
```
